# Optimizing a Trainium2 kernel written in Bass

```python
import numpy as np
import jax
import jax.numpy as jnp

def _softmax(x, axis=-1):
    return jax.nn.softmax(x, axis=axis)

def _gelu(x):
    return jax.nn.gelu(x, approximate=True)

def _silu(x):
    return jax.nn.silu(x)

def _sigmoid(x):
    return jax.nn.sigmoid(x)

def _layernorm(x, axis=-1, eps=1e-05):
    m = jnp.mean(x, axis=axis, keepdims=True)
    v = jnp.var(x, axis=axis, keepdims=True)
    return (x - m) / jnp.sqrt(v + eps)

def _scatter_add(tgt, idx, src, axis=0):
    return tgt.at[idx].add(src)

def _segment_sum(src, seg, n):
    return jax.ops.segment_sum(src, seg, n)
kernel_name = 'mk_decoder_preln_d1_seqx_r4_1d1c9c'

def setup_inputs(seed: int=0):
    np.random.seed(seed)
    _w = jnp.asarray

    def _rec_inputs():
        import jax
        import jax.numpy as jnp
        _rk = jax.random.key(seed)
        x = 0.5 + 0.2887 * jax.random.normal(jax.random.fold_in(_rk, 1), (4, 512, 512), jnp.float32)
        _lenS = 512 - jax.random.randint(jax.random.fold_in(_rk, 7), (4,), 0, max(1, 512 // 4) + 1, jnp.int32)
        _lenS2 = 512 - jax.random.randint(jax.random.fold_in(_rk, 8), (4,), 0, max(1, 512 // 4) + 1, jnp.int32)
        _ctx_512P = jax.random.normal(jax.random.fold_in(_rk, 11), (4, 16, 128), jnp.float32)
        _ctx_512c = jax.random.dirichlet(jax.random.fold_in(_rk, 511), 0.3 * jnp.ones((16,), jnp.float32), (4, 512))
        _ctx_512t = jnp.einsum('bsk,bkd->bsd', _ctx_512c, _ctx_512P)
        _ctx_512t = _ctx_512t * jax.lax.rsqrt(jnp.mean(jnp.square(_ctx_512t)) + 1e-12) * 0.953939
        ctx_512 = -0.000392918 + 0.999932 * (_ctx_512t + 0.3 * jax.random.normal(jax.random.fold_in(_rk, 611), (4, 512, 128), jnp.float32))
        return (x, ctx_512)
    x, ctx_512 = _rec_inputs()

    def _L0_attn_setup():
        import jax, jax.numpy as jnp
        import numpy as np
        import math
        DIM = 512
        N_HEADS = 16
        N_KV_HEADS = 8
        HEAD_DIM = DIM // N_HEADS
        N_REP = N_HEADS // N_KV_HEADS
        BLOCK = 128
        TOPK = 8
        NEG_INF = -10000.0
        SEQ = 1024
        BS = 1

        def _rope_tables(seq_len, head_dim, base=10000.0):
            inv_freq = 1.0 / base ** (jnp.arange(0, head_dim, 2, dtype=jnp.float32) / head_dim)
            ang = jnp.arange(seq_len, dtype=jnp.float32)[:, None] * inv_freq[None, :]
            return (jnp.cos(ang), jnp.sin(ang))

        def _apply_rope(t, cos, sin):
            t1 = t[..., 0::2]
            t2 = t[..., 1::2]
            c = cos[None, :, None, :]
            s = sin[None, :, None, :]
            out_even = t1 * c - t2 * s
            out_odd = t1 * s + t2 * c
            out = jnp.stack([out_even, out_odd], axis=-1)
            return out.reshape(t.shape)
        key = jax.random.key(seed)
        ks = jax.random.split(key, 5)
        scale = 1.0 / math.sqrt(DIM)
        x = jax.random.normal(ks[0], (BS, SEQ, DIM), dtype=jnp.float32)
        wq = jax.random.normal(ks[1], (DIM, N_HEADS * HEAD_DIM), dtype=jnp.float32) * scale
        wk = jax.random.normal(ks[2], (DIM, N_KV_HEADS * HEAD_DIM), dtype=jnp.float32) * scale
        wv = jax.random.normal(ks[3], (DIM, N_KV_HEADS * HEAD_DIM), dtype=jnp.float32) * scale
        wo = jax.random.normal(ks[4], (DIM, DIM), dtype=jnp.float32) * scale
        return {'x': x, 'wq': wq, 'wk': wk, 'wv': wv, 'wo': wo}
    _L0_attn_all = _L0_attn_setup()
    _L0_attn_in = {k: v for k, v in _L0_attn_all.items() if k in ('wq', 'wk', 'wv', 'wo')}
    del _L0_attn_all

    def _L0_xattn_setup():
        import jax, jax.numpy as jnp
        import numpy as np
        B, N, D = (16, 512, 128)
        H = 4
        TOP_K_RATIO = 0.3
        key = jax.random.key(seed)
        k1, k2, k3, k4 = jax.random.split(key, 4)
        h = jax.random.normal(k1, (B, N, D), dtype=jnp.float32)
        adj_raw = jax.random.uniform(k2, (B, N, N), dtype=jnp.float32)
        lim = 1.0 / np.sqrt(D)
        Wq = jax.random.uniform(k3, (D, D), minval=-lim, maxval=lim, dtype=jnp.float32)
        Wk = jax.random.uniform(k4, (D, D), minval=-lim, maxval=lim, dtype=jnp.float32)
        gamma_raw = jnp.float32(-0.85)
        return {'h': h, 'adj_raw': adj_raw, 'Wq': Wq, 'Wk': Wk, 'gamma_raw': gamma_raw}
    _L0_xattn_all = _L0_xattn_setup()
    _L0_xattn_in = {k: v for k, v in _L0_xattn_all.items() if k in ('Wq', 'Wk', 'gamma_raw')}
    del _L0_xattn_all

    def _L0_ffn_setup():
        import jax, jax.numpy as jnp
        import numpy as np
        E, K, H, I, GS = (16, 4, 512, 384, 128)
        B, S = (1, 256)
        FP4_LUT = jnp.array([0.0, 0.5, 1.0, 1.5, 2.0, 3.0, 4.0, 6.0, -0.0, -0.5, -1.0, -1.5, -2.0, -3.0, -4.0, -6.0], jnp.float32)

        def dequant_fp4(packed, scales, gs=GS):
            shifts = jnp.arange(8, dtype=jnp.int32) * 4
            codes = packed[..., :, None, :] >> shifts[:, None] & 15
            w = FP4_LUT[codes]
            new_shape = codes.shape[:-3] + (codes.shape[-3] * 8, codes.shape[-1])
            w = w.reshape(new_shape)
            return w * jnp.repeat(scales, gs, axis=-2)

        def swiglu(h):
            g, u = jnp.split(h, 2, axis=-1)
            return jax.nn.silu(g) * u
        key = jax.random.key(seed)
        ks = jax.random.split(key, 10)

        def packed(k, shape):
            return jax.random.randint(k, shape, 0, 2147483647, dtype=jnp.int32)

        def scale(k, shape):
            return 0.01 + 0.04 * jax.random.uniform(k, shape, dtype=jnp.float32)
        return {'hidden': jax.random.normal(ks[0], (B, S, H), jnp.float32), 'gate_w': jax.random.normal(ks[1], (E, H), jnp.float32) * H ** (-0.5), 'gate_up_packed': packed(ks[2], (E, H // 8, 2 * I)), 'gate_up_scales': scale(ks[3], (E, H // GS, 2 * I)), 'down_packed': packed(ks[4], (E, I // 8, H)), 'down_scales': scale(ks[5], (E, I // GS, H)), 'shared_gate_up_packed': packed(ks[6], (H // 8, 2 * I)), 'shared_gate_up_scales': scale(ks[7], (H // GS, 2 * I)), 'shared_down_packed': packed(ks[8], (I // 8, H)), 'shared_down_scales': scale(ks[9], (I // GS, H))}
    _L0_ffn_all = _L0_ffn_setup()
    _L0_ffn_in = {k: v for k, v in _L0_ffn_all.items() if k in ('gate_w', 'gate_up_packed', 'gate_up_scales', 'down_packed', 'down_scales', 'shared_gate_up_packed', 'shared_gate_up_scales', 'shared_down_packed', 'shared_down_scales')}
    del _L0_ffn_all
    return {'x': x, 'ctx_512': ctx_512, 'L0_attn_wq': _L0_attn_in['wq'], 'L0_attn_wk': _L0_attn_in['wk'], 'L0_attn_wv': _L0_attn_in['wv'], 'L0_attn_wo': _L0_attn_in['wo'], 'L0_xattn_Wq': _L0_xattn_in['Wq'], 'L0_xattn_Wk': _L0_xattn_in['Wk'], 'L0_xattn_gamma_raw': _L0_xattn_in['gamma_raw'], 'L0_ffn_gate_w': _L0_ffn_in['gate_w'], 'L0_ffn_gate_up_packed': _L0_ffn_in['gate_up_packed'], 'L0_ffn_gate_up_scales': _L0_ffn_in['gate_up_scales'], 'L0_ffn_down_packed': _L0_ffn_in['down_packed'], 'L0_ffn_down_scales': _L0_ffn_in['down_scales'], 'L0_ffn_shared_gate_up_packed': _L0_ffn_in['shared_gate_up_packed'], 'L0_ffn_shared_gate_up_scales': _L0_ffn_in['shared_gate_up_scales'], 'L0_ffn_shared_down_packed': _L0_ffn_in['shared_down_packed'], 'L0_ffn_shared_down_scales': _L0_ffn_in['shared_down_scales']}

def reference(x, ctx_512, L0_attn_wq, L0_attn_wk, L0_attn_wv, L0_attn_wo, L0_xattn_Wq, L0_xattn_Wk, L0_xattn_gamma_raw, L0_ffn_gate_w, L0_ffn_gate_up_packed, L0_ffn_gate_up_scales, L0_ffn_down_packed, L0_ffn_down_scales, L0_ffn_shared_gate_up_packed, L0_ffn_shared_gate_up_scales, L0_ffn_shared_down_packed, L0_ffn_shared_down_scales):
    import jax
    import jax.numpy as jnp

    def _L0_attn_ref(x, wq, wk, wv, wo):
        import jax, jax.numpy as jnp
        import numpy as np
        import math
        DIM = 512
        N_HEADS = 16
        N_KV_HEADS = 8
        HEAD_DIM = DIM // N_HEADS
        N_REP = N_HEADS // N_KV_HEADS
        BLOCK = 128
        TOPK = 8
        NEG_INF = -10000.0
        SEQ = 1024
        BS = 1

        def _rope_tables(seq_len, head_dim, base=10000.0):
            inv_freq = 1.0 / base ** (jnp.arange(0, head_dim, 2, dtype=jnp.float32) / head_dim)
            ang = jnp.arange(seq_len, dtype=jnp.float32)[:, None] * inv_freq[None, :]
            return (jnp.cos(ang), jnp.sin(ang))

        def _apply_rope(t, cos, sin):
            t1 = t[..., 0::2]
            t2 = t[..., 1::2]
            c = cos[None, :, None, :]
            s = sin[None, :, None, :]
            out_even = t1 * c - t2 * s
            out_odd = t1 * s + t2 * c
            out = jnp.stack([out_even, out_odd], axis=-1)
            return out.reshape(t.shape)
        bs, S, _ = x.shape
        inv_sqrt_d = 1.0 / math.sqrt(HEAD_DIM)
        q = (x @ wq).reshape(bs, S, N_HEADS, HEAD_DIM)
        k = (x @ wk).reshape(bs, S, N_KV_HEADS, HEAD_DIM)
        v = (x @ wv).reshape(bs, S, N_KV_HEADS, HEAD_DIM)
        cos, sin = _rope_tables(S, HEAD_DIM)
        q = _apply_rope(q, cos, sin)
        k = _apply_rope(k, cos, sin)
        q = jnp.transpose(q, (0, 2, 1, 3))
        k = jnp.transpose(k, (0, 2, 1, 3))
        v = jnp.transpose(v, (0, 2, 1, 3))
        k_e = jnp.repeat(k, N_REP, axis=1)
        v_e = jnp.repeat(v, N_REP, axis=1)
        num_blocks = S // BLOCK
        k_blocks = k_e.reshape(bs, N_HEADS, num_blocks, BLOCK, HEAD_DIM)
        block_means = k_blocks.mean(axis=3)
        gating = jnp.einsum('bhsd,bhnd->bhsn', q, block_means) * inv_sqrt_d
        q_block_idx = jnp.arange(S) // BLOCK
        future_block = q_block_idx[:, None] < jnp.arange(num_blocks)[None, :]
        gating = jnp.where(future_block[None, None], NEG_INF, gating)
        curr_k = min(TOPK, num_blocks)
        _, sel_idx = jax.lax.top_k(gating, curr_k)
        selected = jnp.sum(jax.nn.one_hot(sel_idx, num_blocks, dtype=jnp.float32), axis=-2) > 0
        token_keep = jnp.repeat(selected, BLOCK, axis=-1)[..., :S]
        token_mask = jnp.where(token_keep, 0.0, NEG_INF)
        scores = jnp.einsum('bhsd,bhtd->bhst', q, k_e) * inv_sqrt_d
        causal = jnp.triu(jnp.ones((S, S), dtype=jnp.float32), k=1)
        final_mask = jnp.maximum(token_mask, causal[None, None] * NEG_INF)
        scores = scores + final_mask
        probs = jax.nn.softmax(scores.astype(jnp.float32), axis=-1).astype(scores.dtype)
        out = jnp.einsum('bhst,bhtd->bhsd', probs, v_e)
        out = jnp.transpose(out, (0, 2, 1, 3)).reshape(bs, S, N_HEADS * HEAD_DIM)
        return out @ wo

    def _L0_xattn_ref(h, adj_raw, Wq, Wk, gamma_raw):
        import jax, jax.numpy as jnp
        import numpy as np
        B, N, D = (16, 512, 128)
        H = 4
        TOP_K_RATIO = 0.3
        b, n, dm = h.shape
        d = dm // H
        Q = (h @ Wq.T).reshape(b, n, H, d).transpose(0, 2, 1, 3)
        K = (h @ Wk.T).reshape(b, n, H, d).transpose(0, 2, 1, 3)
        sim = jnp.einsum('bhnd,bhmd->bnm', Q, K) / (jnp.sqrt(jnp.float32(d)) * H)
        k = max(1, int(n * TOP_K_RATIO))
        topk_vals = jax.lax.top_k(sim, k)[0]
        threshold = topk_vals[:, :, -1:]
        sparse_mask = (sim >= threshold).astype(sim.dtype)
        A_learned = jax.nn.sigmoid(sim) * sparse_mask
        A_learned = (A_learned + jnp.swapaxes(A_learned, -1, -2)) * 0.5
        gamma = jax.nn.sigmoid(gamma_raw)
        return (1.0 - gamma) * adj_raw + gamma * A_learned

    def _L0_ffn_ref(hidden, gate_w, gate_up_packed, gate_up_scales, down_packed, down_scales, shared_gate_up_packed, shared_gate_up_scales, shared_down_packed, shared_down_scales):
        import jax, jax.numpy as jnp
        import numpy as np
        E, K, H, I, GS = (16, 4, 512, 384, 128)
        B, S = (1, 256)
        FP4_LUT = jnp.array([0.0, 0.5, 1.0, 1.5, 2.0, 3.0, 4.0, 6.0, -0.0, -0.5, -1.0, -1.5, -2.0, -3.0, -4.0, -6.0], jnp.float32)

        def dequant_fp4(packed, scales, gs=GS):
            shifts = jnp.arange(8, dtype=jnp.int32) * 4
            codes = packed[..., :, None, :] >> shifts[:, None] & 15
            w = FP4_LUT[codes]
            new_shape = codes.shape[:-3] + (codes.shape[-3] * 8, codes.shape[-1])
            w = w.reshape(new_shape)
            return w * jnp.repeat(scales, gs, axis=-2)

        def swiglu(h):
            g, u = jnp.split(h, 2, axis=-1)
            return jax.nn.silu(g) * u
        b, s, h = hidden.shape
        x = hidden.reshape(-1, h)
        probs = jax.nn.softmax(x @ gate_w.T, axis=-1)
        vals, idx = jax.lax.top_k(probs, K)
        w = vals / jnp.sum(vals, axis=-1, keepdims=True)
        combine = jnp.einsum('tke,tk->te', jax.nn.one_hot(idx, E, dtype=x.dtype), w)
        w_gu = dequant_fp4(gate_up_packed, gate_up_scales)
        act = swiglu(jnp.einsum('th,ehi->eti', x, w_gu))
        w_d = dequant_fp4(down_packed, down_scales)
        y_e = jnp.einsum('eti,eih->eth', act, w_d)
        out = jnp.einsum('te,eth->th', combine, y_e)
        act_s = swiglu(x @ dequant_fp4(shared_gate_up_packed, shared_gate_up_scales))
        out = out + act_s @ dequant_fp4(shared_down_packed, shared_down_scales)
        return out.reshape(b, s, h)
    x = x + _L0_attn_ref(_layernorm(x, axis=-1), L0_attn_wq, L0_attn_wk, L0_attn_wv, L0_attn_wo)
    x = x + _L0_xattn_ref(ctx_512, _layernorm(x, axis=-1), L0_xattn_Wq, L0_xattn_Wk, L0_xattn_gamma_raw)
    x = x + _L0_ffn_ref(_layernorm(x, axis=-1), L0_ffn_gate_w, L0_ffn_gate_up_packed, L0_ffn_gate_up_scales, L0_ffn_down_packed, L0_ffn_down_scales, L0_ffn_shared_gate_up_packed, L0_ffn_shared_gate_up_scales, L0_ffn_shared_down_packed, L0_ffn_shared_down_scales)
    return x

_drawn_inputs = setup_inputs


def setup_inputs(seed=0):
    import zlib

    import numpy as np

    out = dict(_drawn_inputs(seed))
    spreads = {}
    factors = {}
    for name, (base, spread) in spreads.items():
        noise = np.random.default_rng([zlib.crc32(name.encode()), seed]).standard_normal(out[name].shape)
        drawn = base * np.exp(spread * noise) if base else spread * noise
        out[name] = jnp.asarray(drawn.astype(out[name].dtype))
    for name, factor in factors.items():
        out[name] = (out[name] * factor).astype(out[name].dtype)
    return out
```

```python
from contextlib import ExitStack

import numpy as np

import concourse.bass as bass
from concourse import mybir
from concourse.alu_op_type import AluOpType as ALU

F32 = mybir.dt.float32
U32 = mybir.dt.uint32
FP8 = mybir.dt.float8e4
ACT = mybir.ActivationFunctionType
AX = mybir.AxisListType

P = 128
B, S, D = 4, 512, 512
TB = S // P
NT = B * TB
KC = D // P
H, G, DH = 16, 8, 32
HP = 4
C = 128
TOPK_SIM = max(1, int(S * 0.3))
ROUNDS = (TOPK_SIM - 1) // 8
SIM_SCALE = 1.0 / (float(np.sqrt(np.float32(C // 4))) * 4)
ATT_SCALE = DH ** -0.5
E, TOPE, I = 16, 4, 384
NE = E + 1
WR = D // 8
GU, DN = 2 * I, D
NW = GU + DN
FP4_SCALE = 64.0
EPS = 1e-5


def by_word(rows):
    return rows.rearrange("p (j r) -> p r j", j=8)


def build_program(nc, x_d, ctx_d, wq_d, wk_d, wv_d, wo_d, xq_d, xk_d, gam_d, gw_d, pk_d, sc_d,
                  cos_d, sin_d, id_d, iota_d, out_d):
    with ExitStack() as ctx:
        x = ctx.enter_context(nc.sbuf_tensor("x", [P, NT, D], F32))
        ident = ctx.enter_context(nc.sbuf_tensor("ident", [P, P], F32))
        comb = ctx.enter_context(nc.sbuf_tensor("comb", [P, NT, NE], F32))
        xr_s = nc.dram_tensor("ffn_rows", [NT * P, D], F32, kind="Internal").ap()
        bank = [ctx.enter_context(nc.psum_tensor(f"bank{i}", [P, 512], F32)) for i in range(8)]
        build_mixers(nc, x, ident, comb, xr_s, bank, x_d, ctx_d, wq_d, wk_d, wv_d, wo_d, xq_d, xk_d,
                     gam_d, gw_d, cos_d, sin_d, id_d, iota_d)
        build_experts(nc, x, ident, comb, xr_s, bank, pk_d, sc_d, out_d)


def build_mixers(nc, x, ident, comb, xr_s, bank, x_d, ctx_d, wq_d, wk_d, wv_d, wo_d, xq_d, xk_d,
                 gam_d, gw_d, cos_d, sin_d, id_d, iota_d):
    with ExitStack() as ctx:
        def sb(name, shape, dt=F32):
            return ctx.enter_context(nc.sbuf_tensor(name, shape, dt))

        def sem(name):
            return ctx.enter_context(nc.semaphore(name))

        def dram(name, shape):
            return nc.dram_tensor(name, shape, F32, kind="Internal").ap()

        qk_s = dram("rope_scratch", [6, P, S])

        iota = sb("iota", [P, E])
        gam = sb("gam", [P, 4])
        wq = sb("wq", [P, KC, 4 * P])
        wk = sb("wk", [P, KC, 2 * P])
        wv = sb("wv", [P, KC, G * DH])
        wo = sb("wo", [P, KC, D])
        xq = sb("xq", [P, C])
        xk = sb("xk", [P, C])
        gw = sb("gw", [P, KC, E])
        cos = sb("cos", [P, S])
        sin = sb("sin", [P, S])
        ctx_t = sb("ctx_t", [P, S])
        xn = sb("xn", [P, TB, D])
        xnT = sb("xnT", [P, KC, S])
        rope_t = sb("rope_t", [P, 4, S])
        rope_o = sb("rope_o", [P, 2, S])
        QT = sb("QT", [DH + 1, H, S])
        KT = sb("KT", [DH + 1, G, S])
        V = sb("V", [P, TB, G, 2 * DH])
        xp = sb("xp", [P, 2, S])
        sim = sb("sim", [P, TB, S])
        work = sb("work", [P, S])
        top8 = sb("top8", [P, TB, 8])
        nm = sb("nm", [P, TB, H])
        nmT = sb("nmT", [H, S])
        prob = sb("prob", [P, 8, S])
        AT = sb("AT", [P, HP, S])
        den = sb("den", [P, 2, S])
        rden = sb("rden", [P, S])
        stats = sb("stats", [P, TB, 6])
        mv = sb("mv", [P, TB, 2])
        ve = sb("ve", [P, TB])
        sd = sb("sd", [P, TB])
        y0 = sb("y0", [P, TB])
        y1 = sb("y1", [P, TB])
        rstd = sb("rstd", [P, TB])
        ln_s = sb("ln_s", [P, TB])
        ln_t = sb("ln_t", [P, TB])
        nl = sb("nl", [P, TB])
        ex = sb("ex", [P, TB, E])
        e8 = sb("e8", [P, TB, 8])
        i8 = sb("i8", [P, TB, 8], U32)
        f8 = sb("f8", [P, TB, 8])
        esum = sb("esum", [P, TB])
        oneh = sb("oneh", [P, E])

        s_const = sem("constants_loaded")
        s_x = sem("x_loaded")
        s_ctx = sem("context_loaded")
        s_init = sem("ones_set")
        s_pass = sem("wait_passed")
        s_ch = sem("vector_chain")
        s_var = sem("variance_ready")
        s_sd = sem("deviation_ready")
        s_gam = sem("gamma_tanh_ready")
        s_xn = sem("rows_normalised")
        s_tr = sem("tiles_transposed")
        s_trc = sem("transposes_copied")
        s_qk = sem("qk_pair_projected")
        s_rope_rd = sem("qk_pair_read")
        s_rope = sem("rope_pair_ready")
        s_roped = sem("rope_pair_stored")
        s_qkld = sem("qk_loaded")
        s_v = sem("v_projected")
        s_vc = sem("v_copied")
        s_xp = sem("context_projected")
        s_xpc = sem("context_copied")
        s_sim = sem("sim_ready")
        s_simc = sem("sim_copied")
        s_S = sem("scores_ready")
        s_mx = sem("scores_max_ready")
        s_mT = sem("max_transposed")
        s_mTc = sem("max_copied")
        s_ml = sem("max_row_loaded")
        s_ST = sem("shifted_scores_ready")
        s_ex = sem("exp_ready")
        s_pv = sem("pv_ready")
        s_den = sem("denominators_copied")
        s_o = sem("outputs_copied")
        s_rd = sem("denominators_used")
        s_at = sem("attention_ready")
        s_op = sem("out_projected")
        s_x1 = sem("x1_ready")
        s_sig = sem("sim_tanh_ready")
        s_adj = sem("adjacency_ready")
        s_adjT = sem("adjacency_transposed")
        s_x2 = sem("x2_ready")
        s_rows = sem("ffn_rows_stored")
        s_lg = sem("logits_ready")
        s_nl = sem("logit_max_ready")
        s_le = sem("logit_exp_ready")
        s_comb = sem("combine_ready")

        block = ctx.enter_context(nc.Block())

        @block.sync
        def _(sp):
            for dst, src in ((ident[:, :], id_d), (wq[:, :, :], wq_d), (wk[:, :, :], wk_d),
                             (wv[:, :, :], wv_d), (cos[:, :], cos_d), (sin[:, :], sin_d),
                             (xq[:, :], xq_d), (xk[:, :], xk_d), (wo[:, :, :], wo_d),
                             (gw[:, :, :], gw_d), (iota[:, :], iota_d),
                             (gam[:, 0:1], gam_d)):
                sp.dma_start(dst, src).then_inc(s_const, 16)
            with sp.Fori(0, B) as b:
                sp.dma_start(ctx_t[:, :], ctx_d[b]).then_inc(s_ctx, 16)
                for p in range(3):
                    sp.wait_ge(s_rope, 3 * b + p + 1)
                    sp.dma_start(qk_s[2 * p:2 * p + 2].rearrange("c p t -> p c t"), rope_o[:, :, :]).then_inc(s_roped, 16)
                sp.wait_ge(s_roped, 48 * (b + 1))
                for r in range(2):
                    for par in range(2):
                        sp.dma_start(QT[par * 16:par * 16 + 16, :, :].rearrange("i (g r) t -> i r g t", r=2)[:, r],
                                     qk_s[2 * r + par].rearrange("(g i) t -> i g t", g=G)).then_inc(s_qkld, 16)
                for par in range(2):
                    sp.dma_start(KT[par * 16:par * 16 + 16, :, :],
                                 qk_s[4 + par].rearrange("(g i) t -> i g t", g=G)).then_inc(s_qkld, 16)
                sp.wait_ge(s_mTc, b + 1)
                sp.dma_start(QT[DH:DH + 1, :, :], nmT[:, :]).then_inc(s_ml, 16)
                sp.wait_ge(s_xn, 8 * b + 8)
                sp.dma_start(xr_s.rearrange("(n p) d -> n p d", p=P)[bass.ds(b * TB, TB)].rearrange("n p d -> p n d"),
                             xn[:, :, :]).then_inc(s_rows, 16)
            sp.wait_ge(s_rows, 16 * B)

        @block.gpsimd
        def _(pool):
            for n in range(NT):
                pool.dma_start(x[:, n, :], x_d[n * P:(n + 1) * P, :]).then_inc(s_x, 16)
            nc.gpsimd.memset(KT[DH:DH + 1, :, :], 1.0).then_inc(s_init, 1)
            pool.wait_ge(s_init, 1)
            nc.gpsimd.memset(V[:, :, :, DH:2 * DH], 1.0).then_inc(s_init, 1)
            nc.gpsimd.memset(comb[:, :, E:NE], FP4_SCALE).then_inc(s_init, 1)

        @block.tensor
        def _(pe):
            pe.wait_ge(s_const, 16 * 12)
            with pe.Fori(0, B) as b:
                def transposes(rnd):
                    for i in range(TB):
                        pe.wait_ge(s_xn, 8 * b + 4 * rnd + i + 1)
                        if rnd or i >= 2:
                            pe.wait_ge(s_trc, 8 * b + 4 * rnd + i - 1)
                        for kc in range(KC):
                            last = nc.tensor.transpose(bank[i % 2][:, kc * P:(kc + 1) * P],
                                                       xn[:, i, kc * P:(kc + 1) * P], ident[:, :])
                        last.then_inc(s_tr, 1)

                transposes(0)
                pe.wait_ge(s_trc, 8 * b + 4)
                for c in range(6):
                    w = wq[:, :, c * P:(c + 1) * P] if c < 4 else wk[:, :, (c - 4) * P:(c - 3) * P]
                    for kc in range(KC):
                        last = nc.tensor.matmul(bank[2 + c][:, :], w[:, kc, :], xnT[:, kc, :],
                                                start=(kc == 0), stop=(kc == KC - 1))
                    if c % 2:
                        last.then_inc(s_qk, 1)
                for i in range(TB):
                    if i >= 2:
                        pe.wait_ge(s_vc, 4 * b + i - 1)
                    for kc in range(KC):
                        last = nc.tensor.matmul(bank[i % 2][:, 0:G * DH], xnT[:, kc, i * P:(i + 1) * P],
                                                wv[:, kc, :], start=(kc == 0), stop=(kc == KC - 1))
                    last.then_inc(s_v, 1)
                pe.wait_ge(s_ctx, 16 * (b + 1))
                for n, w in enumerate((xq, xk)):
                    pe.wait_ge(s_vc, 4 * b + 3 + n)
                    nc.tensor.matmul(bank[n][:, :], w[:, :], ctx_t[:, :], start=True, stop=True).then_inc(s_xp, 1)
                pe.wait_ge(s_xpc, 2 * b + 2)
                for i in range(TB):
                    pe.wait_ge(s_rope_rd, 3 * b + i // 2 + 1)
                    nc.tensor.matmul(bank[2 + i][:, :], xp[:, 0, i * P:(i + 1) * P], xp[:, 1, :],
                                     start=True, stop=True).then_inc(s_sim, 1)
                pe.wait_ge(s_qkld, 16 * 6 * (b + 1))
                pe.wait_ge(s_simc, 4 * b + 4)
                pe.wait_ge(s_rope_rd, 3 * b + 3)
                for h in range(H):
                    for half in range(2):
                        u = 2 * h + half
                        if u >= 3:
                            pe.wait_ge(s_mx, 32 * b + u - 2)
                        for q in range(2):
                            i = 2 * half + q
                            last = nc.tensor.matmul(bank[2 + 2 * (u % 3) + q][:, :],
                                                    QT[0:DH, h, i * P:(i + 1) * P], KT[0:DH, h // 2, :],
                                                    start=True, stop=True)
                        last.then_inc(s_S, 1)
                pe.wait_ge(s_mx, 32 * b + 32)
                for i in range(TB):
                    last = nc.tensor.transpose(bank[0][0:H, i * P:(i + 1) * P], nm[:, i, :], ident[:, :])
                last.then_inc(s_mT, 1)
                pe.wait_ge(s_ml, 16 * (b + 1))

                def shifted_scores(h, kc):
                    u = 4 * h + kc
                    if u >= 4:
                        pe.wait_ge(s_ex, 64 * b + u - 3)
                    nc.tensor.matmul(bank[2 + kc][:, :], KT[:, h // 2, kc * P:(kc + 1) * P],
                                     QT[:, h, :], start=True, stop=True).then_inc(s_ST, 1)

                for kc in range(KC):
                    shifted_scores(0, kc)
                for h in range(H):
                    for kc in range(KC):
                        if h + 1 < H:
                            shifted_scores(h + 1, kc)
                        if kc == 0 and h >= 2:
                            pe.wait_ge(s_den, 16 * b + h - 1)
                            pe.wait_ge(s_o, 16 * b + h - 1)
                        pe.wait_ge(s_ex, 64 * b + 4 * h + kc + 1)
                        last = nc.tensor.matmul(bank[6 + h % 2][0:2 * DH, :], V[:, kc, h // 2, :],
                                                prob[:, (4 * h + kc) % 8, :],
                                                start=(kc == 0), stop=(kc == KC - 1))
                    last.then_inc(s_pv, 1)
                pe.wait_ge(s_at, 4 * b + 4)
                for i in range(TB):
                    for j in range(HP):
                        last = nc.tensor.matmul(bank[2 + i][:, :], AT[:, j, i * P:(i + 1) * P], wo[:, j, :],
                                                start=(j == 0), stop=(j == HP - 1))
                    last.then_inc(s_op, 1)
                pe.wait_ge(s_adj, 4 * b + 4)
                for i in range(TB):
                    pe.wait_ge(s_x1, 4 * b + i + 1)
                    for j in range(TB):
                        last = nc.tensor.transpose(bank[2 + i][:, j * P:(j + 1) * P],
                                                   xn[:, j, i * P:(i + 1) * P], ident[:, :])
                    last.then_inc(s_adjT, 1)
                transposes(1)
                pe.wait_ge(s_trc, 8 * b + 8)
                for i in range(TB):
                    for kc in range(KC):
                        last = nc.tensor.matmul(bank[6][:, i * E:(i + 1) * E], xnT[:, kc, i * P:(i + 1) * P],
                                                gw[:, kc, :], start=(kc == 0), stop=(kc == KC - 1))
                last.then_inc(s_lg, 1)

        def denominators(act, b, h):
            j, q = h // HP, h % HP
            act.wait_ge(s_pv, H * b + h + 1)
            if j >= 2 and q == 0:
                act.wait_ge(s_rd, 4 * b + j - 1)
            nc.scalar.copy(den[q * DH:(q + 1) * DH, j % 2, :],
                           bank[6 + h % 2][DH:2 * DH, :]).then_inc(s_den, 1)

        @block.scalar
        def _(act):
            act.wait_ge(s_const, 16 * 12)
            nc.scalar.activation(gam[:, 1:2], gam[:, 0:1], ACT.Tanh, scale=0.5).then_inc(s_gam, 1)
            with act.Fori(0, B) as b:
                def deviation(rnd):
                    act.wait_ge(s_var, 3 * b + rnd + 1)
                    nc.scalar.activation(sd[:, :], ve[:, :], ACT.Sqrt).then_inc(s_sd, 1)

                def copy_transposes(rnd):
                    for i in range(TB):
                        act.wait_ge(s_tr, 8 * b + 4 * rnd + i + 1)
                        nc.scalar.copy(xnT[:, :, i * P:(i + 1) * P],
                                       bank[i % 2][:, :].rearrange("p (c t) -> p c t", c=KC)).then_inc(s_trc, 1)

                deviation(0)
                copy_transposes(0)
                act.wait_ge(s_init, 3)
                for i in range(TB):
                    act.wait_ge(s_v, 4 * b + i + 1)
                    nc.scalar.copy(V[:, i, :, 0:DH],
                                   bank[i % 2][:, 0:G * DH].rearrange("p (g d) -> p g d", g=G)).then_inc(s_vc, 1)
                for n in range(2):
                    act.wait_ge(s_xp, 2 * b + n + 1)
                    nc.scalar.copy(xp[:, n, :], bank[n][:, :]).then_inc(s_xpc, 1)
                for i in range(TB):
                    act.wait_ge(s_sim, 4 * b + i + 1)
                    nc.scalar.mul(sim[:, i, :], bank[2 + i][:, :], SIM_SCALE).then_inc(s_simc, 1)
                act.wait_ge(s_mT, b + 1)
                nc.scalar.copy(nmT[:, :], bank[0][0:H, :]).then_inc(s_mTc, 1)
                for h in range(H):
                    for kc in range(KC):
                        u = 4 * h + kc
                        act.wait_ge(s_ST, 64 * b + u + 1)
                        if h >= 2:
                            act.wait_ge(s_pv, H * b + h - 1)
                        nc.scalar.activation(prob[:, u % 8, :], bank[2 + kc][:, :], ACT.Exp,
                                             scale=ATT_SCALE).then_inc(s_ex, 1)
                    if h >= 1:
                        denominators(act, b, h - 1)
                denominators(act, b, H - 1)
                act.wait_ge(s_simc, 4 * b + 4)
                for i in range(TB):
                    nc.scalar.activation(xn[:, i, :], sim[:, i, :], ACT.Tanh, scale=0.5).then_inc(s_sig, 1)
                deviation(1)
                deviation(2)
                copy_transposes(1)
                for i in range(TB):
                    act.wait_ge(s_nl, b + 1)
                    last = nc.scalar.activation(ex[:, i, :], bank[6][:, i * E:(i + 1) * E], ACT.Exp,
                                                bias=nl[:, i:i + 1])
                last.then_inc(s_le, 1)

        @block.vector
        def _(dve):
            dve.wait_ge(s_gam, 1)
            nc.vector.tensor_scalar(gam[:, 2:3], gam[:, 1:2], 1.0, 0.125, ALU.add, ALU.mult)
            nc.vector.tensor_scalar(gam[:, 3:4], gam[:, 1:2], -0.5, 0.5, ALU.mult, ALU.add).then_inc(s_gam, 1)
            dve.wait_ge(s_gam, 2)
            dve.wait_ge(s_x, 16 * NT)

            def batch(b, count):
                def link(ins):
                    count[0] += 1
                    ins.then_inc(s_ch, 1)
                    dve.wait_ge(s_ch, count[0])

                def layer_norm_stats(rnd):
                    for i in range(TB):
                        last = nc.vector.bn_stats(stats[:, i, :], x[:, b * TB + i, :])
                    link(last)
                    for i in range(TB):
                        last = nc.vector.bn_aggr(mv[:, i, :], stats[:, i, :])
                    link(last)
                    nc.vector.tensor_scalar(ve[:, :], mv[:, :, 1], EPS, None, ALU.add).then_inc(s_var, 1)
                    dve.wait_ge(s_sd, 3 * b + rnd + 1)
                    link(nc.vector.reciprocal(y0[:, :], sd[:, :]))
                    link(nc.vector.tensor_tensor(y1[:, :], y0[:, :], y0[:, :], ALU.mult))
                    link(nc.vector.tensor_tensor(y1[:, :], y1[:, :], ve[:, :], ALU.mult))
                    link(nc.vector.tensor_scalar(y1[:, :], y1[:, :], -0.5, 1.5, ALU.mult, ALU.add))
                    link(nc.vector.tensor_tensor(rstd[:, :], y1[:, :], y0[:, :], ALU.mult))

                def normalise(nibble_major):
                    for i in range(TB):
                        src, dst = x[:, b * TB + i, :], xn[:, i, :]
                        if nibble_major:
                            src, dst = src.rearrange("p (r j) -> p r j", j=8), by_word(dst)
                        nc.vector.tensor_scalar(dst, src, mv[:, i, 0:1], rstd[:, i:i + 1],
                                                ALU.subtract, ALU.mult).then_inc(s_xn, 1)

                layer_norm_stats(0)
                normalise(False)
                for p in range(3):
                    dve.wait_ge(s_qk, 3 * b + p + 1)
                    ev, od = bank[2 + 2 * p], bank[3 + 2 * p]
                    if p > 0:
                        dve.wait_ge(s_rope, 3 * b + p)
                    nc.vector.tensor_tensor(rope_t[:, 0, :], ev[:, :], cos[:, :], ALU.mult)
                    nc.vector.tensor_tensor(rope_t[:, 1, :], od[:, :], sin[:, :], ALU.mult)
                    nc.vector.tensor_tensor(rope_t[:, 2, :], ev[:, :], sin[:, :], ALU.mult)
                    link(nc.vector.tensor_tensor(rope_t[:, 3, :], od[:, :], cos[:, :], ALU.mult))
                    if p > 0:
                        dve.wait_ge(s_roped, 48 * b + 16 * p)
                    nc.vector.tensor_tensor(rope_o[:, 0, :], rope_t[:, 0, :], rope_t[:, 1, :],
                                            ALU.subtract).then_inc(s_rope_rd, 1)
                    nc.vector.tensor_tensor(rope_o[:, 1, :], rope_t[:, 2, :], rope_t[:, 3, :],
                                            ALU.add).then_inc(s_rope, 1)
                for u in range(2 * H):
                    dve.wait_ge(s_S, 32 * b + u + 1)
                    h, half = u // 2, u % 2
                    for q in range(2):
                        last = nc.vector.tensor_reduce(nm[:, 2 * half + q, h:h + 1], bank[2 + 2 * (u % 3) + q][:, :],
                                                       AX.X, ALU.max, negate=True)
                    last.then_inc(s_mx, 1)
                for j in range(HP):
                    for q in range(HP):
                        for r in range(q * (ROUNDS + 1) // HP, (q + 1) * (ROUNDS + 1) // HP):
                            src = sim[:, j, :] if r == 0 else work[:, :]
                            link(nc.vector.max(top8[:, j, :], src))
                            if r < ROUNDS:
                                link(nc.vector.match_replace(work[:, :], top8[:, j, :], src, -3.0e38))
                        h = HP * j + q
                        dve.wait_ge(s_pv, H * b + h + 1)
                        nc.vector.tensor_copy(AT[q * DH:(q + 1) * DH, j, :], bank[6 + h % 2][0:DH, :]).then_inc(s_o, 1)
                    dve.wait_ge(s_den, H * b + HP * j + HP)
                    nc.vector.reciprocal(rden[:, :], den[:, j % 2, :]).then_inc(s_rd, 1)
                    dve.wait_ge(s_rd, 4 * b + j + 1)
                    dve.wait_ge(s_o, H * b + HP * j + HP)
                    nc.vector.tensor_tensor(AT[:, j, :], AT[:, j, :], rden[:, :], ALU.mult).then_inc(s_at, 1)
                for i in range(TB):
                    dve.wait_ge(s_op, 4 * b + i + 1)
                    nc.vector.tensor_tensor(x[:, b * TB + i, :], x[:, b * TB + i, :], bank[2 + i][:, :],
                                            ALU.add).then_inc(s_x1, 1)
                thr = (TOPK_SIM - 1) % 8
                for i in range(TB):
                    dve.wait_ge(s_sig, 4 * b + i + 1)
                    link(nc.vector.tensor_scalar(xn[:, i, :], xn[:, i, :], 1.0, gam[:, 2:3], ALU.add, ALU.mult))
                    nc.vector.scalar_tensor_tensor(xn[:, i, :], sim[:, i, :], top8[:, i, thr:thr + 1], xn[:, i, :],
                                                   ALU.is_ge, ALU.mult).then_inc(s_adj, 1)
                dve.wait_ge(s_x1, 4 * b + 4)
                dve.sem_inc(s_pass, 1)
                layer_norm_stats(1)
                link(nc.vector.tensor_scalar(ln_s[:, :], rstd[:, :], gam[:, 3:4], None, ALU.mult))
                link(nc.vector.tensor_tensor(ln_t[:, :], mv[:, :, 0], ln_s[:, :], ALU.mult))
                nc.vector.tensor_scalar(ln_t[:, :], ln_t[:, :], -1.0, None, ALU.mult)
                link(nc.vector.tensor_scalar(ln_s[:, :], ln_s[:, :], 1.0, None, ALU.add))
                for i in range(TB):
                    xt = x[:, b * TB + i, :]
                    link(nc.vector.tensor_scalar(xt, xt, ln_s[:, i:i + 1], ln_t[:, i:i + 1], ALU.mult, ALU.add))
                    if i == 0:
                        dve.wait_ge(s_adj, 4 * b + 4)
                    link(nc.vector.tensor_tensor(xt, xt, xn[:, i, :], ALU.add))
                    dve.wait_ge(s_adjT, 4 * b + i + 1)
                    link(nc.vector.tensor_tensor(xt, xt, bank[2 + i][:, :], ALU.add))
                layer_norm_stats(2)
                normalise(True)
                dve.wait_ge(s_lg, b + 1)
                nc.vector.tensor_reduce(nl[:, :], bank[6][:, 0:TB * E].rearrange("p (i e) -> p i e", i=TB),
                                        AX.X, ALU.max, negate=True).then_inc(s_nl, 1)
                dve.wait_ge(s_le, b + 1)
                dve.sem_inc(s_pass, 1)
                for i in range(TB):
                    last = nc.vector.max(e8[:, i, :], ex[:, i, :])
                link(last)
                for i in range(TB):
                    last = nc.vector.max_index(i8[:, i, :], e8[:, i, :], ex[:, i, :])
                link(last)
                nc.vector.tensor_copy(f8[:, :, :], i8[:, :, :])
                link(nc.vector.tensor_reduce(esum[:, :], e8[:, :, 0:TOPE], AX.X, ALU.add))
                link(nc.vector.reciprocal(esum[:, :], esum[:, :]))
                link(nc.vector.tensor_scalar(esum[:, :], esum[:, :], FP4_SCALE, None, ALU.mult))
                for i in range(TB):
                    link(nc.vector.tensor_scalar(e8[:, i, :], e8[:, i, :], esum[:, i:i + 1], None, ALU.mult))
                    cb = comb[:, b * TB + i, 0:E]
                    link(nc.vector.tensor_scalar(cb, iota[:, :], f8[:, i, 0:1], e8[:, i, 0:1], ALU.is_equal, ALU.mult))
                    for k in range(1, TOPE):
                        link(nc.vector.tensor_scalar(oneh[:, :], iota[:, :], f8[:, i, k:k + 1], e8[:, i, k:k + 1],
                                                     ALU.is_equal, ALU.mult))
                        link(nc.vector.tensor_tensor(cb, cb, oneh[:, :], ALU.add))
                dve.wait_ge(s_roped, 48 * (b + 1))
                dve.wait_ge(s_tr, 8 * (b + 1))
                dve.wait_ge(s_rows, 16 * (b + 1))

            with dve.Fori(0, B) as b:
                dve.sem_clear(s_ch)
                batch(b, [0])



PIECES = 8
PW = NW // PIECES


def build_experts(nc, x, ident, comb, xr_s, bank, pk_d, sc_d, out_d):
    with ExitStack() as ctx:
        def sb(name, shape, dt=F32):
            return ctx.enter_context(nc.sbuf_tensor(name, shape, dt))

        def sem(name):
            return ctx.enter_context(nc.semaphore(name))

        pk = sb("packed", [P, 2, NW], U32)
        sc = sb("scales", [P, 2, NW])
        mag = sb("magnitude", [P, PW], U32)
        sgn = sb("sign", [P, PW], U32)
        dec = sb("codes_fp8", [P, PW], U32)
        val = sb("code_values", [P, 4, PW])
        W = sb("W", [P, 2, 4, NW])
        rows = sb("rows", [P, 2, D])
        xT = sb("xT", [P, 2, D])
        sg = sb("silu", [P, 2, I])
        act_r = sb("act_rows", [P, 2, D])
        aT = sb("aT", [P, 2, D])
        yt = sb("y_weighted", [P, 2, D])

        s_pk = sem("expert_loaded")
        s_zero = sem("act_tail_zeroed")
        s_pass = sem("wait_passed")
        s_dch = sem("decode_chain")
        s_dec = sem("piece_decoded")
        s_val = sem("piece_converted")
        s_W = sem("piece_scaled")
        s_row = [sem("even_rows_loaded"), sem("odd_rows_loaded")]
        s_tx = sem("rows_transposed")
        s_xT = sem("rows_T_copied")
        s_gu = sem("gate_up_ready")
        s_sg = sem("silu_ready")
        s_act = sem("act_ready")
        s_ta = sem("act_transposed")
        s_aT = sem("act_T_copied")
        s_dn = sem("down_ready")
        s_y = sem("y_weighted_ready")
        s_add = sem("y_added")
        s_out = sem("out_stored")

        N = NE * NT
        rows_d = xr_s.rearrange("(n p) d -> n p d", p=P)

        block = ctx.enter_context(nc.Block())

        @block.sync
        def _(sp):
            def load_expert(e):
                for hf in range(2):
                    sp.dma_start(pk[hf * WR:(hf + 1) * WR, e % 2, :], pk_d[e]).then_inc(s_pk, 16)
                    sp.dma_start(sc[hf * WR:(hf + 1) * WR, e % 2, :], sc_d[e]).then_inc(s_pk, 16)

            def load_rows(n, u):
                sp.dma_start(rows[:, u, :], rows_d[n % NT]).then_inc(s_row[u], 16)

            def next_rows(e, tp):
                for u in range(2):
                    n = e * NT + 2 * tp + u
                    sp.wait_ge(s_tx, n + 1)
                    load_rows(n + 2, u)

            load_expert(0)
            load_rows(0, 0)
            load_rows(1, 1)
            sp.wait_ge(s_pk, 64)
            load_expert(1)
            with sp.Fori(0, NE - 2) as e:
                sp.wait_ge(s_W, PIECES * (e + 1))
                sp.wait_ge(s_pk, 64 * (e + 2))
                load_expert(e + 2)
                with sp.Fori(0, NT // 2) as tp:
                    next_rows(e, tp)
            with sp.Fori(0, NT // 2) as tp:
                next_rows(NE - 2, tp)
            with sp.Fori(0, NT // 2 - 1) as tp:
                next_rows(NE - 1, tp)

            sp.wait_ge(s_add, N)
            sp.dma_start(out_d.rearrange("(n p) d -> p n d", p=P), x[:, :, :]).then_inc(s_out, 16)
            sp.wait_ge(s_out, 16)

        @block.gpsimd
        def _(pool):
            nc.gpsimd.memset(act_r[:, :, :], 0.0).then_inc(s_zero, 1)

            def scale_piece(e, k, first=False):
                pool.wait_ge(s_dec, PIECES * e + k + 1)
                if not first:
                    pool.wait_ge(s_W, PIECES * e + k)
                pool.sem_inc(s_pass, 1)
                nc.gpsimd.tensor_copy(val[:, :, :], dec[:, :].bitcast(FP8).rearrange("p (n b) -> p b n", b=4)) \
                    .then_inc(s_val, 1)
                pool.wait_ge(s_val, PIECES * e + k + 1)
                pool.sem_inc(s_pass, 1)
                s = sc[:, e % 2, bass.ds(k * PW, PW)].rearrange("p (o n) -> p o n", o=1).broadcast_to([P, 4, PW])
                nc.gpsimd.tensor_tensor(W[:, e % 2, :, bass.ds(k * PW, PW)], val[:, :, :], s, ALU.mult) \
                    .then_inc(s_W, 1)

            def add_y(n, u):
                pool.wait_ge(s_y, n + 1)
                pool.sem_inc(s_pass, 1)
                xt = x[:, n % NT, :]
                nc.gpsimd.tensor_tensor(xt, xt, yt[:, u, :], ALU.add).then_inc(s_add, 1)

            scale_piece(0, 0, first=True)
            with pool.Fori(1, PIECES) as k:
                scale_piece(0, k)
            with pool.Fori(0, NE - 1) as e:
                with pool.Fori(0, NT // 2) as tp:
                    scale_piece(e + 1, tp)
                    for u in range(2):
                        add_y(e * NT + tp * 2 + u, u)
            with pool.Fori(0, NT // 2) as tp:
                for u in range(2):
                    add_y((NE - 1) * NT + tp * 2 + u, u)

        @block.vector
        def _(dve):
            def decode_piece(e, k, first=False):
                dve.sem_clear(s_dch)
                cols = bass.ds(k * PW, PW)
                hi = pk[WR:P, e % 2, cols]
                dve.wait_ge(s_pk, 64 * (e + 1))
                nc.vector.tensor_scalar(hi, hi, 4, None, ALU.logical_shift_right).then_inc(s_dch, 1)
                dve.wait_ge(s_dch, 1)
                src = pk[:, e % 2, cols]
                nc.vector.tensor_scalar(mag[:, :], src, 2, 0x1C1C1C1C, ALU.logical_shift_left, ALU.bitwise_and)
                nc.vector.tensor_scalar(sgn[:, :], src, 4, 0x80808080, ALU.logical_shift_left,
                                        ALU.bitwise_and).then_inc(s_dch, 1)
                dve.wait_ge(s_dch, 2)
                if not first:
                    dve.wait_ge(s_val, PIECES * e + k)
                nc.vector.tensor_tensor(dec[:, :], mag[:, :], sgn[:, :], ALU.bitwise_or).then_inc(s_dec, 1)

            def gate_times_up(n, u):
                dve.wait_ge(s_sg, n + 1)
                nc.vector.scalar_tensor_tensor(by_word(act_r[:, u, :])[:, 0:I // 8, :],
                                               bank[4 + u][:, 0:I].rearrange("p (r j) -> p r j", j=8), FP4_SCALE,
                                               sg[:, u, :].rearrange("p (r j) -> p r j", j=8),
                                               ALU.mult, ALU.mult).then_inc(s_act, 1)

            decode_piece(0, 0, first=True)
            with dve.Fori(1, PIECES) as k:
                decode_piece(0, k)
            dve.wait_ge(s_zero, 1)
            with dve.Fori(0, NE - 1) as e:
                with dve.Fori(0, NT // 2) as tp:
                    decode_piece(e + 1, tp)
                    for u in range(2):
                        gate_times_up(e * NT + tp * 2 + u, u)
            with dve.Fori(0, NT // 2) as tp:
                for u in range(2):
                    gate_times_up((NE - 1) * NT + tp * 2 + u, u)

        @block.scalar
        def _(act):
            def copy_xT(n, u):
                act.wait_ge(s_tx, n + 1)
                nc.scalar.copy(xT[:, u, :], bank[0][:, :]).then_inc(s_xT, 1)

            def silu(n, u):
                act.wait_ge(s_gu, n + 1)
                nc.scalar.activation(sg[:, u, :], bank[2 + u][:, 0:I], ACT.Silu, scale=FP4_SCALE).then_inc(s_sg, 1)

            def copy_aT(n, u):
                act.wait_ge(s_ta, n + 1)
                nc.scalar.copy(aT[:, u, :], bank[1][:, :]).then_inc(s_aT, 1)

            def weight_y(n, u, first=False):
                act.wait_ge(s_dn, n + 1)
                if not first:
                    act.wait_ge(s_add, n - 1)
                nc.scalar.activation(yt[:, u, :], bank[6 + u][:, :], ACT.Copy,
                                     scale=comb[:, n % NT, bass.ds(n // NT, 1)]).then_inc(s_y, 1)

            copy_xT(0, 0)
            copy_xT(1, 1)
            silu(0, 0)

            def pair(m, first=False):
                for u in (1, 0):
                    n = 2 * m + 2 - u
                    copy_xT(n + 1, 1 - u)
                    copy_aT(n - 1, 1 - u)
                    silu(n, u)
                    weight_y(n - 1, 1 - u, first)

            pair(0, first=True)
            with act.Fori(1, (N - 2) // 2) as m:
                pair(m)
            copy_aT(N - 2, 0)
            silu(N - 1, 1)
            weight_y(N - 2, 0)
            copy_aT(N - 1, 1)
            weight_y(N - 1, 1)

        @block.tensor
        def _(pe):
            def transpose_rows(n, u, first=False):
                pe.wait_ge(s_row[u], 16 * (n // 2 + 1))
                if not first:
                    pe.wait_ge(s_xT, n)
                for b in range(4):
                    last = nc.tensor.transpose(bank[0][:, b * P:(b + 1) * P], rows[:, u, b * P:(b + 1) * P], ident[:, :])
                last.then_inc(s_tx, 1)

            def gate_up(n, u, first=False):
                pe.wait_ge(s_xT, n + 1)
                pe.wait_ge(s_W, PIECES * (n // NT + 1))
                if not first:
                    pe.wait_ge(s_act, n - 1)
                for half in range(2):
                    for b in range(4):
                        last = nc.tensor.matmul(bank[2 + 2 * half + u][:, 0:I], xT[:, u, b * P:(b + 1) * P],
                                                W[:, (n // NT) % 2, b, half * I:(half + 1) * I],
                                                start=(b == 0), stop=(b == 3))
                last.then_inc(s_gu, 1)

            def transpose_act(n, u, first=False):
                pe.wait_ge(s_act, n + 1)
                if not first:
                    pe.wait_ge(s_aT, n)
                for b in range(4):
                    last = nc.tensor.transpose(bank[1][:, b * P:(b + 1) * P], act_r[:, u, b * P:(b + 1) * P], ident[:, :])
                last.then_inc(s_ta, 1)

            def down(n, u, first=False):
                pe.wait_ge(s_aT, n + 1)
                if not first:
                    pe.wait_ge(s_y, n - 1)
                for b in range(4):
                    last = nc.tensor.matmul(bank[6 + u][:, :], aT[:, u, b * P:(b + 1) * P],
                                            W[:, (n // NT) % 2, b, GU:NW], start=(b == 0), stop=(b == 3))
                last.then_inc(s_dn, 1)

            transpose_rows(0, 0, first=True)
            transpose_rows(1, 1)
            gate_up(0, 0, first=True)

            def pair(m, first=False):
                for u in (1, 0):
                    n = 2 * m + 2 - u
                    transpose_rows(n + 1, 1 - u)
                    transpose_act(n - 1, 1 - u, first and u == 1)
                    gate_up(n, u)
                    down(n - 1, 1 - u, first)

            pair(0, first=True)
            with pe.Fori(1, (N - 2) // 2) as m:
                pair(m)
            transpose_act(N - 2, 0)
            gate_up(N - 1, 1)
            down(N - 2, 0)
            transpose_act(N - 1, 1)
            down(N - 1, 1)


def kernel(x, ctx_512, L0_attn_wq, L0_attn_wk, L0_attn_wv, L0_attn_wo, L0_xattn_Wq, L0_xattn_Wk,
           L0_xattn_gamma_raw, L0_ffn_gate_w, L0_ffn_gate_up_packed, L0_ffn_gate_up_scales,
           L0_ffn_down_packed, L0_ffn_down_scales, L0_ffn_shared_gate_up_packed,
           L0_ffn_shared_gate_up_scales, L0_ffn_shared_down_packed, L0_ffn_shared_down_scales):
    import concourse.bacc as bacc
    from concourse.bass_utils import run_bass_kernel_spmd

    A = np.asarray

    def lhs(w):
        return np.ascontiguousarray(w.reshape(KC, P, -1).transpose(1, 0, 2))

    wq = A(L0_attn_wq).reshape(D, G, 2, DH // 2, 2).transpose(0, 2, 4, 1, 3).reshape(D, H * DH)
    wk = A(L0_attn_wk).reshape(D, G, DH // 2, 2).transpose(0, 3, 1, 2).reshape(D, G * DH)

    def with_shared(routed, shared):
        return np.concatenate([A(routed), A(shared)[None]], axis=0)

    def pad_rows(w):
        out = np.zeros((w.shape[0], WR, w.shape[2]), w.dtype)
        out[:, :w.shape[1]] = w
        return out

    packed = np.concatenate([with_shared(L0_ffn_gate_up_packed, L0_ffn_shared_gate_up_packed),
                             pad_rows(with_shared(L0_ffn_down_packed, L0_ffn_shared_down_packed))], axis=2)
    scales = np.concatenate([
        np.repeat(with_shared(L0_ffn_gate_up_scales, L0_ffn_shared_gate_up_scales), P // 8, axis=1),
        pad_rows(np.repeat(with_shared(L0_ffn_down_scales, L0_ffn_shared_down_scales), P // 8, axis=1))], axis=2)

    inv = (1.0 / np.float32(10000.0) ** (np.arange(0, DH, 2, dtype=np.float32) / DH)).astype(np.float32)
    ang = inv[:, None] * np.arange(S, dtype=np.float32)[None, :]
    arrays = {
        "x": A(x).reshape(NT * P, D),
        "ctxT": np.ascontiguousarray(A(ctx_512).transpose(0, 2, 1)),
        "wq": lhs(wq), "wk": lhs(wk), "wv": lhs(A(L0_attn_wv)), "wo": lhs(A(L0_attn_wo)),
        "xWq": np.ascontiguousarray(A(L0_xattn_Wq).T), "xWk": np.ascontiguousarray(A(L0_xattn_Wk).T),
        "gamma": np.broadcast_to(A(L0_xattn_gamma_raw).reshape(1, 1), (P, 1)).copy(),
        "gate": lhs(A(L0_ffn_gate_w).T.reshape(WR, 8, E).transpose(1, 0, 2)),
        "packed": packed.view(np.uint32), "scales": scales,
        "cos": np.tile(np.cos(ang), (G, 1)).astype(np.float32),
        "sin": np.tile(np.sin(ang), (G, 1)).astype(np.float32),
        "ident": np.eye(P, dtype=np.float32),
        "iota": np.tile(np.arange(E, dtype=np.float32), (P, 1)),
    }
    nc = bacc.Bacc("TRN2", target_bir_lowering=False, num_devices=1)
    aps = [nc.dram_tensor(f"in_{k}", v.shape, mybir.dt.from_np(v.dtype), kind="ExternalInput").ap()
           for k, v in arrays.items()]
    out = nc.dram_tensor("out", (NT * P, D), F32, kind="ExternalOutput").ap()
    build_program(nc, *aps, out)
    r = run_bass_kernel_spmd(nc, [{f"in_{k}": v for k, v in arrays.items()}], core_ids=[0])
    return r.results[0]["out"].reshape(B, S, D)
```

```python
from contextlib import ExitStack

import numpy as np

import concourse.bass as bass
from concourse import mybir
from concourse.alu_op_type import AluOpType as ALU

F32 = mybir.dt.float32
BF16 = mybir.dt.bfloat16
U32 = mybir.dt.uint32
I32 = mybir.dt.int32
FP8 = mybir.dt.float8e4
ACT = mybir.ActivationFunctionType
AX = mybir.AxisListType

P = 128
B, S, D = 4, 512, 512
TB = S // P
NT = B * TB
KC = D // P
H, G, DH = 16, 8, 32
HP = 4
C = 128
TOPK_SIM = max(1, int(S * 0.3))
ROUNDS = (TOPK_SIM - 1) // 8
SIM_SCALE = 1.0 / (float(np.sqrt(np.float32(C // 4))) * 4)
ATT_SCALE = DH ** -0.5
E, TOPE, I = 16, 4, 384
NE = E + 1
WR = D // 8
GU, DN = 2 * I, D
NW = GU + DN
RT = NT * P * TOPE // P + E
ALL = RT + NT
RG = NT * P + P
FP4_SCALE = 64.0
EPS = 1e-5


def by_word(rows):
    return rows.rearrange("p (j r) -> p r j", j=8)


def build_program(nc, x_d, ctx_d, wq_d, wk_d, wv_d, wo_d, xq_d, xk_d, gam_d, gw_d, pk_d, sc_d,
                  cos_d, sin_d, id_d, tri_d, cst_d, out_d):
    with ExitStack() as ctx:
        x = ctx.enter_context(nc.sbuf_tensor("x", [P, NT, D], F32))
        ident = ctx.enter_context(nc.sbuf_tensor("ident", [P, P], F32))
        def keep(name, shape, dt=F32):
            return ctx.enter_context(nc.sbuf_tensor(name, shape, dt))

        wt = keep("expert_weights", [P, NT, TOPE])
        ysl = keep("result_slots", [P, NT, TOPE], U32)
        tile_x = keep("tile_rows", [1, ALL], I32)
        tile_e = keep("tile_experts", [1, ALL], I32)
        tend = keep("expert_ends", [1, E], I32)
        xg_s = nc.dram_tensor("expert_rows", [E * RG + NT * P, D], F32, kind="Internal").ap()
        y_s = nc.dram_tensor("expert_results", [RT * P, D], F32, kind="Internal").ap()
        banks = ctx.enter_context(nc.psum_tensor("banks", [P, 8, 512], F32))
        bank = [banks[:, i, :] for i in range(8)]
        build_mixers(nc, x, ident, wt, ysl, tile_x, tile_e, tend, xg_s, banks, bank, x_d, ctx_d, wq_d, wk_d,
                     wv_d, wo_d, xq_d, xk_d, gam_d, gw_d, cos_d, sin_d, id_d, tri_d, cst_d)
        build_experts(nc, x, ident, wt, ysl, tile_x, tile_e, tend, xg_s, y_s, bank, pk_d, sc_d, out_d)


IOTA, M128, REG, PAD, LE, JV, TAIL = 0, 16, 32, 48, 64, 320, 320 + RT
NCST = TAIL + NT


def build_mixers(nc, x, ident, wt, ysl, tile_x, tile_e, tend, xg_s, banks, bank, x_d, ctx_d, wq_d, wk_d,
                 wv_d, wo_d, xq_d, xk_d, gam_d, gw_d, cos_d, sin_d, id_d, tri_d, cst_d):
    with ExitStack() as ctx:
        def sb(name, shape, dt=F32):
            return ctx.enter_context(nc.sbuf_tensor(name, shape, dt))

        def sem(name):
            return ctx.enter_context(nc.semaphore(name))

        q_s = nc.dram_tensor("q_parts", [3, DH, H, S], BF16, kind="Internal").ap()
        k_s = nc.dram_tensor("k_parts", [3, DH, G, S], BF16, kind="Internal").ap()

        tri = sb("earlier", [P, P])
        ones = sb("ones", [P, P])
        cst = sb("cst", [P, NCST])
        gam = sb("gam", [P, 4])
        wq = sb("wq", [P, KC, 4 * P])
        wk = sb("wk", [P, KC, 2 * P])
        wv = sb("wv", [P, KC, G * DH])
        wo = sb("wo", [P, KC, D])
        xq = sb("xq", [P, C])
        xk = sb("xk", [P, C])
        gw = sb("gw", [P, KC, E])
        cos = sb("cos", [P, S])
        sin = sb("sin", [P, S])
        ctx_t = sb("ctx_t", [P, S])
        xn = sb("xn", [P, TB, D])
        xnT = sb("xnT", [P, KC, S])
        rope_t = sb("rope_t", [P, 4, S])
        xf = rope_t
        rope_o = sb("rope_o", [P, 2, S])
        Q1 = sb("Q1", [P, H, S], BF16)
        K1 = sb("K1", [P, G, S], BF16)
        Q2 = sb("Q2", [2 * DH + 2, H, S], BF16)
        K2 = sb("K2", [2 * DH + 2, G, S], BF16)
        V = sb("V", [P, TB, G, 2 * DH])
        xp = sb("xp", [P, 2, S])
        sim = sb("sim", [P, TB, S])
        work = sb("work", [P, S])
        top8 = sb("top8", [P, TB, 8])
        nm = sb("nm", [P, TB, H])
        nmT = sb("nmT", [H, 2, S], BF16)
        prob = sb("prob", [P, 8, S])
        flat = prob[:, :, :].rearrange("p a b -> p (a b)")
        part = flat[:, 0:6 * S].bitcast(BF16).rearrange("p (u c a t) -> p u c a t", u=2, c=3, a=2)
        rest = flat[:, 6 * S:8 * S].rearrange("p (a t) -> p a t", a=2)
        AT = sb("AT", [P, HP, S])
        den = sb("den", [P, 2, S])
        rden = sb("rden", [P, S])
        stats = sb("stats", [P, TB, 6])
        mv = sb("mv", [P, TB, 2])
        ve = sb("ve", [P, TB])
        sd = sb("sd", [P, TB])
        y0 = sb("y0", [P, TB])
        y1 = sb("y1", [P, TB])
        rstd = sb("rstd", [P, TB])
        ln_s = sb("ln_s", [P, TB])
        ln_t = sb("ln_t", [P, TB])
        nl = sb("nl", [P, TB])
        ex = sb("ex", [P, TB, E])
        e8 = sb("e8", [P, TB, 8])
        i8 = sb("i8", [P, TB, 8], U32)
        f8 = sb("f8", [P, TB, 8])
        esum = sb("esum", [P, TB])
        ei = sb("expert_index", [P, NT, TOPE])
        xsl = sb("row_slots", [P, NT, TOPE])
        slot = sb("batch_slots", [P, TB, TOPE], U32)
        oneh = sb("oneh", [P, TB, TOPE, E])
        routed = sb("routed", [P, TB, E])
        run = sb("routed_before", [P, TB + 1, E])
        posx = sb("posx", [P, TB, E])
        cnt = sb("cnt", [P, E])
        nt = sb("nt", [P, E])
        te = sb("te", [P, E])
        dlt = sb("dlt", [P, E])
        big = AT[:, :, :].rearrange("p a b -> p (a b)")[:, 0:RT * E].rearrange("p (j e) -> p j e", e=E)
        big2 = prob[:, :, :].rearrange("p a b -> p (a b)")[:, 0:RT * E].rearrange("p (j e) -> p j e", e=E)
        zeros = work
        cj = sb("cj", [P, RT])
        sj = sb("sj", [P, RT])
        xj = sb("xj", [P, RT])
        padi = sb("padi", [P, E], U32)

        s_const = sem("constants_loaded")
        s_x = sem("x_loaded")
        s_ctx = sem("context_loaded")
        s_init = sem("ones_set")
        s_pass = sem("wait_passed")
        s_ch = sem("vector_chain")
        s_var = sem("variance_ready")
        s_sd = sem("deviation_ready")
        s_gam = sem("gamma_tanh_ready")
        s_xn = sem("rows_normalised")
        s_tr = sem("tiles_transposed")
        s_trc = sem("transposes_copied")
        s_qk = sem("qk_pair_projected")
        s_rope_rd = sem("qk_pair_read")
        s_rope = sem("rope_pair_ready")
        s_hi = sem("first_part_ready")
        s_rest = sem("rest_ready")
        s_mid = sem("second_part_ready")
        s_low = sem("third_part_ready")
        s_roped = [sem(f"parts_stored_{p}") for p in range(3)]
        s_qkld = sem("qk_loaded")
        s_v = sem("v_projected")
        s_vc = sem("v_copied")
        s_xp = sem("context_projected")
        s_xpc = sem("context_copied")
        s_sim = sem("sim_ready")
        s_simc = sem("sim_copied")
        s_S = sem("scores_ready")
        s_mx = sem("scores_max_ready")
        s_mT = sem("max_transposed")
        s_mTc = sem("max_copied")
        s_mTm = sem("max_remainder_ready")
        s_ml = sem("max_row_loaded")
        s_ST = sem("shifted_scores_ready")
        s_ex = sem("exp_ready")
        s_pv = sem("pv_ready")
        s_den = sem("denominators_copied")
        s_o = sem("outputs_copied")
        s_rd = sem("denominators_used")
        s_at = sem("attention_ready")
        s_op = sem("out_projected")
        s_x1 = sem("x1_ready")
        s_sig = sem("sim_tanh_ready")
        s_adj = sem("adjacency_ready")
        s_adjT = sem("adjacency_transposed")
        s_x2 = sem("x2_ready")
        s_rows = sem("ffn_rows_stored")
        s_lg = sem("logits_ready")
        s_nl = sem("logit_max_ready")
        s_le = sem("logit_exp_ready")
        s_one = sem("one_hot_ready")
        s_pos = sem("positions_ready")
        s_slot = sem("slots_ready")
        s_scat = sem("rows_scattered")
        s_free = sem("row_buffer_free")
        s_cnt = sem("counts_ready")
        s_pad = sem("pad_slots_ready")
        s_padd = sem("pads_scattered")

        block = ctx.enter_context(nc.Block())

        @block.sync
        def _(sp):
            for dst, src in ((ident[:, :], id_d), (wq[:, :, :], wq_d), (wk[:, :, :], wk_d),
                             (wv[:, :, :], wv_d), (cos[:, :], cos_d), (sin[:, :], sin_d),
                             (xq[:, :], xq_d), (xk[:, :], xk_d), (wo[:, :, :], wo_d),
                             (gw[:, :, :], gw_d), (tri[:, :], tri_d), (cst[:, :], cst_d),
                             (gam[:, 0:1], gam_d)):
                sp.dma_start(dst, src).then_inc(s_const, 16)
            with sp.Fori(0, B) as b:
                sp.dma_start(ctx_t[:, :], ctx_d[b]).then_inc(s_ctx, 16)
                for p in range(3):
                    sp.wait_ge(s_low, 3 * b + p + 1)
                    for c in range(3):
                        for par in range(2):
                            dst = (k_s[c] if p == 2 else q_s[c].rearrange("d (g r) t -> r d g t", r=2)[p])
                            sp.dma_start(dst[par * 16:par * 16 + 16].rearrange("i g t -> g i t"),
                                         part[:, p % 2, c, par]).then_inc(s_roped[p], 16)
                for p in range(3):
                    sp.wait_ge(s_roped[p], 96 * (b + 1))
                for dst, c in ((Q1[0:32], 0), (Q1[32:64], 1), (Q1[64:96], 0), (Q1[96:128], 1),
                               (Q2[0:32], 2), (Q2[32:64], 0)):
                    sp.dma_start(dst, q_s[c]).then_inc(s_qkld, 16)
                for dst, c in ((K1[0:32], 0), (K1[32:64], 0), (K1[64:96], 1), (K1[96:128], 1),
                               (K2[0:32], 0), (K2[32:64], 2)):
                    sp.dma_start(dst, k_s[c]).then_inc(s_qkld, 16)
                sp.wait_ge(s_mTm, b + 1)
                for c in range(2):
                    sp.dma_start(Q2[2 * DH + c:2 * DH + c + 1, :, :], nmT[:, c, :]).then_inc(s_ml, 16)
                sp.wait_ge(s_xn, 8 * b + 8)
                sp.dma_start(xg_s[bass.ds(E * RG + b * TB * P, TB * P)].rearrange("(n p) d -> p n d", p=P),
                             xf[:, :, :]).then_inc(s_rows, 16)
            sp.wait_ge(s_rows, 16 * B)

        @block.gpsimd
        def _(pool):
            for n in range(NT):
                pool.dma_start(x[:, n, :], x_d[n * P:(n + 1) * P, :]).then_inc(s_x, 16)
            nc.gpsimd.memset(K2[2 * DH:2 * DH + 2, :, :], 1.0).then_inc(s_init, 1)
            pool.wait_ge(s_init, 1)
            nc.gpsimd.memset(V[:, :, :, DH:2 * DH], 1.0).then_inc(s_init, 1)
            pool.wait_ge(s_init, 2)
            nc.gpsimd.memset(ones[:, :], 1.0).then_inc(s_init, 1)
            nc.gpsimd.memset(run[:, 0, :], 0.0).then_inc(s_init, 1)
            pool.wait_ge(s_init, 4)
            pool.sem_inc(s_free, 1)
            with pool.Fori(0, B) as b:
                for p in range(3):
                    if p > 0:
                        pool.wait_ge(s_low, 3 * b + p)
                    pool.wait_ge(s_hi, 3 * b + p + 1)
                    nc.gpsimd.tensor_tensor(rest, rope_o[:, :, :], part[:, p % 2, 0], ALU.subtract).then_inc(s_rest, 1)
                    pool.wait_ge(s_mid, 3 * b + p + 1)
                    nc.gpsimd.tensor_tensor(part[:, p % 2, 2], rest, part[:, p % 2, 1], ALU.subtract) \
                        .then_inc(s_low, 1)
                for j in range(HP):
                    pool.wait_ge(s_rd, 4 * b + j + 1)
                    pool.wait_ge(s_o, H * b + HP * j + HP)
                    nc.gpsimd.tensor_tensor(AT[:, j, :], AT[:, j, :], rden[:, :], ALU.mult).then_inc(s_at, 1)
                pool.wait_ge(s_slot, b + 1)
                pool.sem_inc(s_pass, 1)
                for i in range(TB):
                    for k in range(TOPE):
                        pool.indirect_dma_start(xg_s, bass.IndirectOffsetOnAxis(slot[:, i, k:k + 1], 0),
                                                xf[:, i, :], None).then_inc(s_scat, 16)
                pool.wait_ge(s_scat, 16 * TB * TOPE * (b + 1))
                pool.wait_ge(s_rows, 16 * (b + 1))
                pool.sem_inc(s_free, 1)
            pool.wait_ge(s_pad, 1)
            for e in range(E):
                pool.indirect_dma_start(xg_s, bass.IndirectOffsetOnAxis(padi[:, e:e + 1], 0), zeros[:, :],
                                        None).then_inc(s_padd, 16)
            pool.wait_ge(s_padd, 16 * E)

        @block.tensor
        def _(pe):
            pe.wait_ge(s_const, 16 * 13)
            with pe.Fori(0, B) as b:
                def transposes(rnd):
                    rows = xf if rnd else xn
                    for i in range(TB):
                        pe.wait_ge(s_xn, 8 * b + 4 * rnd + i + 1)
                        if rnd or i >= 2:
                            pe.wait_ge(s_trc, 8 * b + 4 * rnd + i - 1)
                        for kc in range(KC):
                            last = nc.tensor.transpose(bank[i % 2][:, kc * P:(kc + 1) * P],
                                                       rows[:, i, kc * P:(kc + 1) * P], ident[:, :])
                        last.then_inc(s_tr, 1)

                transposes(0)
                pe.wait_ge(s_trc, 8 * b + 4)
                for c in range(6):
                    w = wq[:, :, c * P:(c + 1) * P] if c < 4 else wk[:, :, (c - 4) * P:(c - 3) * P]
                    for kc in range(KC):
                        last = nc.tensor.matmul(bank[2 + c][:, :], w[:, kc, :], xnT[:, kc, :],
                                                start=(kc == 0), stop=(kc == KC - 1))
                    if c % 2:
                        last.then_inc(s_qk, 1)
                for i in range(TB):
                    if i >= 2:
                        pe.wait_ge(s_vc, 4 * b + i - 1)
                    for kc in range(KC):
                        last = nc.tensor.matmul(bank[i % 2][:, 0:G * DH], xnT[:, kc, i * P:(i + 1) * P],
                                                wv[:, kc, :], start=(kc == 0), stop=(kc == KC - 1))
                    last.then_inc(s_v, 1)
                pe.wait_ge(s_ctx, 16 * (b + 1))
                for n, w in enumerate((xq, xk)):
                    pe.wait_ge(s_vc, 4 * b + 3 + n)
                    nc.tensor.matmul(bank[n][:, :], w[:, :], ctx_t[:, :], start=True, stop=True).then_inc(s_xp, 1)
                pe.wait_ge(s_xpc, 2 * b + 2)
                for i in range(TB):
                    pe.wait_ge(s_rope_rd, 3 * b + i // 2 + 1)
                    nc.tensor.matmul(bank[2 + i][:, :], xp[:, 0, i * P:(i + 1) * P], xp[:, 1, :],
                                     start=True, stop=True).then_inc(s_sim, 1)
                pe.wait_ge(s_qkld, 16 * 12 * (b + 1))
                pe.wait_ge(s_simc, 4 * b + 4)
                pe.wait_ge(s_rope_rd, 3 * b + 3)
                for h in range(H):
                    for half in range(2):
                        u = 2 * h + half
                        if u >= 3:
                            pe.wait_ge(s_mx, 32 * b + u - 2)
                        for q in range(2):
                            i = 2 * half + q
                            last = nc.tensor.matmul(bank[2 + 2 * (u % 3) + q][:, :],
                                                    Q1[:, h, i * P:(i + 1) * P], K1[:, h // 2, :],
                                                    start=True, stop=True)
                        last.then_inc(s_S, 1)
                pe.wait_ge(s_mx, 32 * b + 32)
                for i in range(TB):
                    last = nc.tensor.transpose(bank[0][0:H, i * P:(i + 1) * P], nm[:, i, :], ident[:, :])
                last.then_inc(s_mT, 1)
                pe.wait_ge(s_ml, 32 * (b + 1))

                def shifted_scores(h, kc):
                    u = 4 * h + kc
                    if u >= 4:
                        pe.wait_ge(s_ex, 64 * b + u - 3)
                    nc.tensor.matmul(bank[2 + kc][:, :], K1[:, h // 2, kc * P:(kc + 1) * P],
                                     Q1[:, h, :], start=True, stop=False)
                    nc.tensor.matmul(bank[2 + kc][:, :], K2[:, h // 2, kc * P:(kc + 1) * P],
                                     Q2[:, h, :], start=False, stop=True).then_inc(s_ST, 1)

                for kc in range(KC):
                    shifted_scores(0, kc)
                for h in range(H):
                    for kc in range(KC):
                        if h + 1 < H:
                            shifted_scores(h + 1, kc)
                        if kc == 0 and h >= 2:
                            pe.wait_ge(s_den, 16 * b + h - 1)
                            pe.wait_ge(s_o, 16 * b + h - 1)
                        pe.wait_ge(s_ex, 64 * b + 4 * h + kc + 1)
                        last = nc.tensor.matmul(bank[6 + h % 2][0:2 * DH, :], V[:, kc, h // 2, :],
                                                prob[:, (4 * h + kc) % 8, :],
                                                start=(kc == 0), stop=(kc == KC - 1))
                    last.then_inc(s_pv, 1)
                pe.wait_ge(s_at, 4 * b + 4)
                for i in range(TB):
                    for j in range(HP):
                        last = nc.tensor.matmul(bank[2 + i][:, :], AT[:, j, i * P:(i + 1) * P], wo[:, j, :],
                                                start=(j == 0), stop=(j == HP - 1))
                    last.then_inc(s_op, 1)
                pe.wait_ge(s_adj, 4 * b + 4)
                for i in range(TB):
                    pe.wait_ge(s_x1, 4 * b + i + 1)
                    for j in range(TB):
                        last = nc.tensor.transpose(bank[2 + i][:, j * P:(j + 1) * P],
                                                   xn[:, j, i * P:(i + 1) * P], ident[:, :])
                    last.then_inc(s_adjT, 1)
                transposes(1)
                pe.wait_ge(s_trc, 8 * b + 8)
                for i in range(TB):
                    for kc in range(KC):
                        last = nc.tensor.matmul(bank[6][:, i * E:(i + 1) * E], xnT[:, kc, i * P:(i + 1) * P],
                                                gw[:, kc, :], start=(kc == 0), stop=(kc == KC - 1))
                last.then_inc(s_lg, 1)
                pe.wait_ge(s_one, b + 1)
                pos = bank[7][:, 0:TB * E]
                nc.tensor.matmul(pos, tri[:, :], routed[:, :, :].rearrange("p i e -> p (i e)"),
                                 start=True, stop=False)
                nc.tensor.matmul(pos, ones[:, :], run[:, 0:TB, :].rearrange("p i e -> p (i e)"),
                                 start=False, stop=True).then_inc(s_pos, 1)
            pe.wait_ge(s_slot, B)
            nc.tensor.matmul(bank[6][:, 0:E], ones[:, :], run[:, 0, :], start=True, stop=True).then_inc(s_cnt, 1)

        def denominators(act, b, h):
            j, q = h // HP, h % HP
            act.wait_ge(s_pv, H * b + h + 1)
            if j >= 2 and q == 0:
                act.wait_ge(s_rd, 4 * b + j - 1)
            nc.scalar.copy(den[q * DH:(q + 1) * DH, j % 2, :],
                           bank[6 + h % 2][DH:2 * DH, :]).then_inc(s_den, 1)
            nc.scalar.copy(AT[q * DH:(q + 1) * DH, j, :], bank[6 + h % 2][0:DH, :]).then_inc(s_o, 1)

        @block.scalar
        def _(act):
            act.wait_ge(s_const, 16 * 13)
            nc.scalar.activation(gam[:, 1:2], gam[:, 0:1], ACT.Tanh, scale=0.5).then_inc(s_gam, 1)
            with act.Fori(0, B) as b:
                def deviation(rnd):
                    act.wait_ge(s_var, 3 * b + rnd + 1)
                    nc.scalar.activation(sd[:, :], ve[:, :], ACT.Sqrt).then_inc(s_sd, 1)

                def copy_transposes(rnd):
                    for i in range(TB):
                        act.wait_ge(s_tr, 8 * b + 4 * rnd + i + 1)
                        nc.scalar.copy(xnT[:, :, i * P:(i + 1) * P],
                                       bank[i % 2][:, :].rearrange("p (c t) -> p c t", c=KC)).then_inc(s_trc, 1)

                deviation(0)
                copy_transposes(0)
                act.wait_ge(s_init, 4)

                def copy_v(i):
                    act.wait_ge(s_v, 4 * b + i + 1)
                    nc.scalar.copy(V[:, i, :, 0:DH],
                                   bank[i % 2][:, 0:G * DH].rearrange("p (g d) -> p g d", g=G)).then_inc(s_vc, 1)

                for p in range(3):
                    act.wait_ge(s_rope, 3 * b + p + 1)
                    if p == 2:
                        act.wait_ge(s_roped[0], 96 * (b + 1))
                    nc.scalar.copy(part[:, p % 2, 0], rope_o[:, :, :]).then_inc(s_hi, 1)
                    act.wait_ge(s_rest, 3 * b + p + 1)
                    nc.scalar.copy(part[:, p % 2, 1], rest).then_inc(s_mid, 1)
                    if p < 2:
                        copy_v(2 * p)
                        copy_v(2 * p + 1)
                for n in range(2):
                    act.wait_ge(s_xp, 2 * b + n + 1)
                    nc.scalar.copy(xp[:, n, :], bank[n][:, :]).then_inc(s_xpc, 1)
                for i in range(TB):
                    act.wait_ge(s_sim, 4 * b + i + 1)
                    nc.scalar.mul(sim[:, i, :], bank[2 + i][:, :], SIM_SCALE).then_inc(s_simc, 1)
                act.wait_ge(s_mT, b + 1)
                nc.scalar.copy(nmT[:, 0, :], bank[0][0:H, :]).then_inc(s_mTc, 1)
                for h in range(H):
                    for kc in range(KC):
                        u = 4 * h + kc
                        act.wait_ge(s_ST, 64 * b + u + 1)
                        if h >= 2:
                            act.wait_ge(s_pv, H * b + h - 1)
                        nc.scalar.activation(prob[:, u % 8, :], bank[2 + kc][:, :], ACT.Exp,
                                             scale=ATT_SCALE).then_inc(s_ex, 1)
                    if h >= 1:
                        denominators(act, b, h - 1)
                denominators(act, b, H - 1)
                act.wait_ge(s_simc, 4 * b + 4)
                for i in range(TB):
                    nc.scalar.activation(xn[:, i, :], sim[:, i, :], ACT.Tanh, scale=0.5).then_inc(s_sig, 1)
                deviation(1)
                deviation(2)
                copy_transposes(1)
                for i in range(TB):
                    act.wait_ge(s_nl, b + 1)
                    last = nc.scalar.activation(ex[:, i, :], bank[6][:, i * E:(i + 1) * E], ACT.Exp,
                                                bias=nl[:, i:i + 1])
                last.then_inc(s_le, 1)

        @block.vector
        def _(dve):
            dve.wait_ge(s_gam, 1)
            nc.vector.tensor_scalar(gam[:, 2:3], gam[:, 1:2], 1.0, 0.125, ALU.add, ALU.mult)
            nc.vector.tensor_scalar(gam[:, 3:4], gam[:, 1:2], -0.5, 0.5, ALU.mult, ALU.add).then_inc(s_gam, 1)
            dve.wait_ge(s_gam, 2)
            dve.wait_ge(s_x, 16 * NT)

            def over(t, n):
                if len(t.shape) == 2:
                    return t.rearrange("p (i k) -> p i k", k=1).broadcast_to([P, t.shape[1], n])
                return t.rearrange("p i (k e) -> p i k e", e=1).broadcast_to([P, t.shape[1], t.shape[2], n])

            def batch(b, count):
                def link(ins):
                    count[0] += 1
                    ins.then_inc(s_ch, 1)
                    dve.wait_ge(s_ch, count[0])

                def layer_norm_stats(rnd):
                    for i in range(TB):
                        last = nc.vector.bn_stats(stats[:, i, :], x[:, b * TB + i, :])
                    link(last)
                    for i in range(TB):
                        last = nc.vector.bn_aggr(mv[:, i, :], stats[:, i, :])
                    link(last)
                    nc.vector.tensor_scalar(ve[:, :], mv[:, :, 1], EPS, None, ALU.add).then_inc(s_var, 1)
                    dve.wait_ge(s_sd, 3 * b + rnd + 1)
                    link(nc.vector.reciprocal(y0[:, :], sd[:, :]))
                    link(nc.vector.tensor_tensor(y1[:, :], y0[:, :], y0[:, :], ALU.mult))
                    link(nc.vector.tensor_tensor(y1[:, :], y1[:, :], ve[:, :], ALU.mult))
                    link(nc.vector.tensor_scalar(y1[:, :], y1[:, :], -0.5, 1.5, ALU.mult, ALU.add))
                    link(nc.vector.tensor_tensor(rstd[:, :], y1[:, :], y0[:, :], ALU.mult))

                def normalise(nibble_major):
                    for i in range(TB):
                        src, dst = x[:, b * TB + i, :], xn[:, i, :]
                        if nibble_major:
                            src, dst = src.rearrange("p (r j) -> p r j", j=8), by_word(xf[:, i, :])
                        nc.vector.tensor_scalar(dst, src, mv[:, i, 0:1], rstd[:, i:i + 1],
                                                ALU.subtract, ALU.mult).then_inc(s_xn, 1)

                layer_norm_stats(0)
                normalise(False)
                for p in range(3):
                    dve.wait_ge(s_qk, 3 * b + p + 1)
                    if p == 0:
                        dve.wait_ge(s_free, b + 1)
                    ev, od = bank[2 + 2 * p], bank[3 + 2 * p]
                    if p > 0:
                        dve.wait_ge(s_rope, 3 * b + p)
                    nc.vector.tensor_tensor(rope_t[:, 0, :], ev[:, :], cos[:, :], ALU.mult)
                    nc.vector.tensor_tensor(rope_t[:, 1, :], od[:, :], sin[:, :], ALU.mult)
                    nc.vector.tensor_tensor(rope_t[:, 2, :], ev[:, :], sin[:, :], ALU.mult)
                    link(nc.vector.tensor_tensor(rope_t[:, 3, :], od[:, :], cos[:, :], ALU.mult))
                    if p > 0:
                        dve.wait_ge(s_rest, 3 * b + p)
                    nc.vector.tensor_tensor(rope_o[:, 0, :], rope_t[:, 0, :], rope_t[:, 1, :],
                                            ALU.subtract).then_inc(s_rope_rd, 1)
                    nc.vector.tensor_tensor(rope_o[:, 1, :], rope_t[:, 2, :], rope_t[:, 3, :],
                                            ALU.add).then_inc(s_rope, 1)
                for u in range(2 * H):
                    dve.wait_ge(s_S, 32 * b + u + 1)
                    h, half = u // 2, u % 2
                    c = 2 + 2 * (u % 3)
                    nc.vector.tensor_reduce(nm[:, 2 * half:2 * half + 2, h], banks[:, c:c + 2, :],
                                            AX.X, ALU.max, negate=True).then_inc(s_mx, 1)
                dve.wait_ge(s_mTc, b + 1)
                nc.vector.tensor_tensor(nmT[:, 1, :], bank[0][0:H, :], nmT[:, 0, :], ALU.subtract).then_inc(s_mTm, 1)
                for j in range(HP):
                    for q in range(HP):
                        for r in range(q * (ROUNDS + 1) // HP, (q + 1) * (ROUNDS + 1) // HP):
                            src = sim[:, j, :] if r == 0 else work[:, :]
                            link(nc.vector.max(top8[:, j, :], src))
                            if r < ROUNDS:
                                link(nc.vector.match_replace(work[:, :], top8[:, j, :], src, -3.0e38))
                    dve.wait_ge(s_den, H * b + HP * j + HP)
                    if j > 0:
                        dve.wait_ge(s_at, 4 * b + j)
                    nc.vector.reciprocal(rden[:, :], den[:, j % 2, :]).then_inc(s_rd, 1)
                for i in range(TB):
                    dve.wait_ge(s_op, 4 * b + i + 1)
                    nc.vector.tensor_tensor(x[:, b * TB + i, :], x[:, b * TB + i, :], bank[2 + i][:, :],
                                            ALU.add).then_inc(s_x1, 1)
                thr = (TOPK_SIM - 1) % 8
                for i in range(TB):
                    dve.wait_ge(s_sig, 4 * b + i + 1)
                    link(nc.vector.tensor_scalar(xn[:, i, :], xn[:, i, :], 1.0, gam[:, 2:3], ALU.add, ALU.mult))
                    nc.vector.scalar_tensor_tensor(xn[:, i, :], sim[:, i, :], top8[:, i, thr:thr + 1], xn[:, i, :],
                                                   ALU.is_ge, ALU.mult).then_inc(s_adj, 1)
                dve.wait_ge(s_x1, 4 * b + 4)
                dve.sem_inc(s_pass, 1)
                layer_norm_stats(1)
                link(nc.vector.tensor_scalar(ln_s[:, :], rstd[:, :], gam[:, 3:4], None, ALU.mult))
                link(nc.vector.tensor_tensor(ln_t[:, :], mv[:, :, 0], ln_s[:, :], ALU.mult))
                nc.vector.tensor_scalar(ln_t[:, :], ln_t[:, :], -1.0, None, ALU.mult)
                link(nc.vector.tensor_scalar(ln_s[:, :], ln_s[:, :], 1.0, None, ALU.add))
                for i in range(TB):
                    xt = x[:, b * TB + i, :]
                    link(nc.vector.tensor_scalar(xt, xt, ln_s[:, i:i + 1], ln_t[:, i:i + 1], ALU.mult, ALU.add))
                    if i == 0:
                        dve.wait_ge(s_adj, 4 * b + 4)
                    link(nc.vector.tensor_tensor(xt, xt, xn[:, i, :], ALU.add))
                    dve.wait_ge(s_adjT, 4 * b + i + 1)
                    link(nc.vector.tensor_tensor(xt, xt, bank[2 + i][:, :], ALU.add))
                layer_norm_stats(2)
                normalise(True)
                dve.wait_ge(s_lg, b + 1)
                nc.vector.tensor_reduce(nl[:, :], bank[6][:, 0:TB * E].rearrange("p (i e) -> p i e", i=TB),
                                        AX.X, ALU.max, negate=True).then_inc(s_nl, 1)
                dve.wait_ge(s_le, b + 1)
                dve.sem_inc(s_pass, 1)
                for i in range(TB):
                    last = nc.vector.max(e8[:, i, :], ex[:, i, :])
                link(last)
                for i in range(TB):
                    last = nc.vector.max_index(i8[:, i, :], e8[:, i, :], ex[:, i, :])
                link(last)
                link(nc.vector.tensor_copy(f8[:, :, :], i8[:, :, :]))
                link(nc.vector.tensor_reduce(esum[:, :], e8[:, :, 0:TOPE], AX.X, ALU.add))
                link(nc.vector.reciprocal(esum[:, :], esum[:, :]))
                link(nc.vector.tensor_scalar(esum[:, :], esum[:, :], FP4_SCALE, None, ALU.mult))
                nc.vector.tensor_tensor(wt[:, bass.ds(b * TB, TB), :], e8[:, :, 0:TOPE],
                                        over(esum[:, :], TOPE), ALU.mult)
                nc.vector.tensor_copy(ei[:, bass.ds(b * TB, TB), :], f8[:, :, 0:TOPE])
                iota = cst[:, IOTA:IOTA + E].rearrange("p (i k e) -> p i k e", i=1, k=1).broadcast_to([P, TB, TOPE, E])
                link(nc.vector.tensor_tensor(oneh[:, :, :, :], iota, over(f8[:, :, 0:TOPE], E), ALU.is_equal))
                link(nc.vector.tensor_reduce(routed[:, :, :], oneh[:, :, :, :].rearrange("p i k e -> p i e k"),
                                             AX.X, ALU.add))
                for i in range(TB):
                    ins = nc.vector.tensor_tensor(run[:, i + 1, :], run[:, i, :], routed[:, i, :], ALU.add)
                    if i < TB - 1:
                        link(ins)
                ins.then_inc(s_one, 1)
                dve.wait_ge(s_pos, b + 1)
                regs = cst[:, REG:REG + E].rearrange("p (i e) -> p i e", i=1).broadcast_to([P, TB, E])
                link(nc.vector.tensor_tensor(posx[:, :, :], bank[7][:, 0:TB * E].rearrange("p (i e) -> p i e", i=TB),
                                             regs, ALU.add))
                link(nc.vector.tensor_tensor(
                    oneh[:, :, :, :], oneh[:, :, :, :],
                    posx[:, :, :].rearrange("p i (k e) -> p i k e", k=1).broadcast_to([P, TB, TOPE, E]), ALU.mult))
                link(nc.vector.tensor_reduce(f8[:, :, 0:TOPE], oneh[:, :, :, :], AX.X, ALU.add))
                link(nc.vector.tensor_copy(xsl[:, bass.ds(b * TB, TB), :], f8[:, :, 0:TOPE]))
                link(nc.vector.tensor_copy(run[:, 0, :], run[:, TB, :]))
                nc.vector.tensor_copy(slot[:, :, :], f8[:, :, 0:TOPE]).then_inc(s_slot, 1)

            with dve.Fori(0, B) as b:
                dve.sem_clear(s_ch)
                batch(b, [0])

            dve.sem_clear(s_ch)
            count = [0]

            def link(ins):
                count[0] += 1
                ins.then_inc(s_ch, 1)
                dve.wait_ge(s_ch, count[0])

            def first(t, m, n):
                return t.rearrange("p (m n) -> p m n", m=1).broadcast_to([P, m, n])

            dve.wait_ge(s_cnt, 1)
            nc.vector.memset(zeros[:, :], 0.0)
            link(nc.vector.tensor_copy(cnt[:, :], bank[6][:, 0:E]))
            link(nc.vector.tensor_tensor(dlt[:, :], cnt[:, :], cst[:, PAD:PAD + E], ALU.add))
            nc.vector.tensor_copy(padi[:, :], dlt[:, :]).then_inc(s_pad, 1)
            link(nc.vector.tensor_tensor(big[:, 0:E, :], over(cnt[:, :], E), first(cst[:, M128:M128 + E], E, E),
                                         ALU.is_gt))
            link(nc.vector.tensor_reduce(nt[:, :], big[:, 0:E, :], AX.X, ALU.add))
            link(nc.vector.tensor_scalar(nt[:, :], nt[:, :], 1.0, None, ALU.max))
            link(nc.vector.tensor_tensor(big[:, 0:E, :], first(nt[:, :], E, E),
                                         cst[:, LE:LE + E * E].rearrange("p (a b) -> p a b", a=E), ALU.mult))
            link(nc.vector.tensor_reduce(te[:, :], big[:, 0:E, :], AX.X, ALU.add))
            nc.vector.tensor_copy(tend[:, :], te[0:1, :])
            link(nc.vector.tensor_tensor(big[:, :, :], first(te[:, :], RT, E), over(cst[:, JV:JV + RT], E),
                                         ALU.is_le))
            link(nc.vector.tensor_reduce(cj[:, :], big[:, :, :], AX.X, ALU.add))
            link(nc.vector.tensor_tensor(big2[:, :, :], big[:, :, :], first(nt[:, :], RT, E), ALU.mult))
            link(nc.vector.tensor_reduce(sj[:, :], big2[:, :, :], AX.X, ALU.add))
            link(nc.vector.tensor_tensor(sj[:, :], cst[:, JV:JV + RT], sj[:, :], ALU.subtract))
            link(nc.vector.tensor_scalar(sj[:, :], sj[:, :], float(P), None, ALU.mult))
            link(nc.vector.tensor_scalar(xj[:, :], cj[:, :], float(RG), None, ALU.mult))
            link(nc.vector.tensor_tensor(xj[:, :], xj[:, :], sj[:, :], ALU.add))
            nc.vector.tensor_copy(tile_x[:, 0:RT], xj[0:1, :])
            nc.vector.tensor_copy(tile_x[:, RT:ALL], cst[0:1, TAIL:TAIL + NT])
            nc.vector.tensor_scalar(tile_e[:, 0:RT], cj[0:1, :], float(E - 1), None, ALU.min)
            nc.vector.memset(tile_e[:, RT:ALL], E)
            link(nc.vector.tensor_tensor(dlt[:, :], te[:, :], nt[:, :], ALU.subtract))
            link(nc.vector.tensor_scalar(dlt[:, :], dlt[:, :], float(P), None, ALU.mult))
            link(nc.vector.tensor_tensor(dlt[:, :], dlt[:, :], cst[:, REG:REG + E], ALU.subtract))
            NK = NT * TOPE
            eis = ei[:, :, :].rearrange("p n k -> p (n k)")
            link(nc.vector.tensor_tensor(big[:, 0:NK, :], first(cst[:, IOTA:IOTA + E], NK, E), over(eis, E),
                                         ALU.is_equal))
            link(nc.vector.tensor_tensor(big[:, 0:NK, :], big[:, 0:NK, :], first(dlt[:, :], NK, E), ALU.mult))
            link(nc.vector.tensor_reduce(cj[:, 0:NK], big[:, 0:NK, :], AX.X, ALU.add))
            nc.vector.tensor_tensor(ysl[:, :, :].rearrange("p n k -> p (n k)"), cj[:, 0:NK],
                                    xsl[:, :, :].rearrange("p n k -> p (n k)"), ALU.add)



def build_experts(nc, x, ident, wt, ysl, tile_x, tile_e, tend, xg_s, y_s, bank, pk_d, sc_d, out_d):
    with ExitStack() as ctx:
        def sb(name, shape, dt=F32):
            return ctx.enter_context(nc.sbuf_tensor(name, shape, dt))

        def sem(name):
            return ctx.enter_context(nc.semaphore(name))

        words = sb("words", [P, NE, NW], U32)
        mag = sb("magnitude", [P, NW], U32)
        cod = sb("codes", [P, NW], U32)
        sc = sb("scales", [P, 2, NW])
        W = sb("W", [P, 2, 4, NW])
        rows = sb("rows", [P, 2, D])
        xT = sb("xT", [P, 2, D])
        sg = sb("silu", [P, 2, I])
        act_r = sb("act_rows", [P, 2, D])
        aT = sb("aT", [P, 2, D])
        yt = sb("y_rows", [P, 2, D])
        yg = W[:, 1, :, :].rearrange("p b n -> p (b n)")[:, 0:2 * TOPE * D].rearrange(
            "p (u k d) -> p u k d", u=2, k=TOPE)
        gi = sb("gather_slots", [P, 2, TOPE], U32)

        s_pk = [sem(f"words_loaded_{q}") for q in range(4)]
        s_zero = sem("act_tail_zeroed")
        s_pass = sem("wait_passed")
        s_dch = sem("decode_chain")
        s_dec = sem("expert_decoded")
        s_sc = [sem("even_scales_loaded"), sem("odd_scales_loaded")]
        s_cod = sem("codes_copied")
        s_W = sem("expert_scaled")
        s_row = [sem("even_rows_loaded"), sem("odd_rows_loaded")]
        s_tx = sem("rows_transposed")
        s_xT = sem("rows_T_copied")
        s_gu = sem("gate_up_ready")
        s_sg = sem("silu_ready")
        s_act = sem("act_ready")
        s_ta = sem("act_transposed")
        s_aT = sem("act_T_copied")
        s_dn = sem("down_ready")
        s_y = sem("y_copied")
        s_st = [sem("even_y_stored"), sem("odd_y_stored")]
        s_gi = sem("gather_slots_copied")
        s_ga = [sem("even_gathered"), sem("odd_gathered")]
        s_cch = sem("gathered_chain")
        s_cmb = sem("gathered_added")
        s_sh = sem("shared_added")
        s_out = sem("out_stored")

        XMAX = E * RG + NT * P - P

        block = ctx.enter_context(nc.Block())

        @block.sync
        def _(sp):
            def load_words(e, q):
                for hf in range(2):
                    sp.dma_start(words[hf * WR:(hf + 1) * WR, e, :], pk_d[e]).then_inc(s_pk[q], 16)

            def load_rows(j, u):
                r = sp.value_load(tile_x[0:1, bass.ds(j, 1)], min_val=0, max_val=XMAX)
                sp.dma_start(rows[:, u, :], xg_s[bass.ds(r, P)]).then_inc(s_row[u], 16)

            def store_y(j, u):
                sp.wait_ge(s_y, j + 1)
                sp.dma_start(y_s.rearrange("(j p) d -> j p d", p=P)[j], yt[:, u, :]).then_inc(s_st[u], 16)

            load_words(0, 0)
            load_rows(0, 0)
            load_rows(1, 1)
            load_words(1, 1)
            load_words(2, 2)
            for e in range(3, NE):
                load_words(e, 3)
            sp.wait_ge(s_tx, 1)
            load_rows(2, 0)
            with sp.Fori(0, RT // 2 - 1) as m:
                for u in (1, 0):
                    j = 2 * m + 2 - u
                    sp.wait_ge(s_tx, j + 1)
                    sp.sem_inc(s_pass, 1)
                    load_rows(j + 2, u)
                    store_y(j - 1, 1 - u)
            sp.wait_ge(s_tx, RT)
            load_rows(RT + 1, 1)
            store_y(RT - 2, 0)
            sp.wait_ge(s_tx, RT + 1)
            load_rows(RT + 2, 0)
            store_y(RT - 1, 1)
            for j in range(RT + 1, ALL - 2):
                sp.wait_ge(s_tx, j + 1)
                load_rows(j + 2, j % 2)
            sp.wait_ge(s_cmb, NT)
            sp.wait_ge(s_sh, NT)
            sp.dma_start(out_d.rearrange("(n p) d -> p n d", p=P), x[:, :, :]).then_inc(s_out, 16)
            sp.wait_ge(s_out, 16)

        @block.gpsimd
        def _(pool):
            nc.gpsimd.memset(act_r[:, :, :], 0.0).then_inc(s_zero, 1)

            def load_scales(e, u):
                for hf in range(2):
                    pool.dma_start(sc[hf * WR:(hf + 1) * WR, u, :], sc_d[e]).then_inc(s_sc[u], 16)

            def scale_expert(e, u, first=False):
                pool.wait_ge(s_dec, e + 1)
                pool.sem_inc(s_pass, 1)
                nc.gpsimd.tensor_copy(cod[:, :], words[:, e, :]).then_inc(s_cod, 1)
                if not first:
                    r = pool.value_load(tend[0:1, bass.ds(e - 2, 1)], min_val=1, max_val=RT)
                    pool.wait_ge(s_dn, r)
                pool.wait_ge(s_cod, e + 1)
                pool.wait_ge(s_sc[u], 32 * (e // 2 + 1))
                pool.sem_inc(s_pass, 1)
                codes = cod[:, :].bitcast(FP8).rearrange("p (n b) -> p b n", b=4)
                for b in range(4):
                    last = nc.gpsimd.tensor_tensor(W[:, u, b, :], codes[:, b], sc[:, u, :], ALU.mult)
                last.then_inc(s_W, 1)
                pool.wait_ge(s_W, e + 1)
                pool.sem_inc(s_pass, 1)

            load_scales(0, 0)
            load_scales(1, 1)
            for e in range(2):
                scale_expert(e, e, first=True)
                load_scales(e + 2, e)
            with pool.Fori(1, E // 2 - 1) as m:
                for u in range(2):
                    scale_expert(2 * m + u, u)
                    load_scales(2 * m + u + 2, u)
            scale_expert(E - 2, 0)
            load_scales(E, 0)
            scale_expert(E - 1, 1)
            scale_expert(E, 0)

            for u in range(2):
                pool.wait_ge(s_st[u], 16 * (RT // 2))

            def gather(n, u, first=False):
                if not first:
                    pool.wait_ge(s_cmb, n - 1)
                    pool.sem_inc(s_pass, 1)
                nc.gpsimd.tensor_copy(gi[:, u, :], ysl[:, n, :]).then_inc(s_gi, 1)
                pool.wait_ge(s_gi, n + 1)
                pool.sem_inc(s_pass, 1)
                for k in range(TOPE):
                    pool.indirect_dma_start(yg[:, u, k], None, y_s,
                                            bass.IndirectOffsetOnAxis(gi[:, u, k:k + 1], 0)).then_inc(s_ga[u], 16)

            gather(0, 0, first=True)
            gather(1, 1, first=True)
            with pool.Fori(1, NT // 2) as m:
                for u in range(2):
                    gather(2 * m + u, u)

        @block.vector
        def _(dve):
            def decode(e, q, loads):
                dve.wait_ge(s_pk[q], loads)
                dve.sem_clear(s_dch)
                hi = words[WR:P, e, :]
                nc.vector.tensor_scalar(hi, hi, 4, None, ALU.logical_shift_right).then_inc(s_dch, 1)
                dve.wait_ge(s_dch, 1)
                w = words[:, e, :]
                nc.vector.tensor_scalar(mag[:, :], w, 2, 0x1C1C1C1C, ALU.logical_shift_left,
                                        ALU.bitwise_and).then_inc(s_dch, 1)
                dve.wait_ge(s_dch, 2)
                nc.vector.tensor_scalar(w, w, 4, 0x80808080, ALU.logical_shift_left,
                                        ALU.bitwise_and).then_inc(s_dch, 1)
                dve.wait_ge(s_dch, 3)
                nc.vector.tensor_tensor(w, w, mag[:, :], ALU.bitwise_or).then_inc(s_dec, 1)

            def gate_times_up(j, u):
                dve.wait_ge(s_sg, j + 1)
                nc.vector.scalar_tensor_tensor(by_word(act_r[:, u, :])[:, 0:I // 8, :],
                                               bank[4 + u][:, 0:I].rearrange("p (r j) -> p r j", j=8), FP4_SCALE,
                                               sg[:, u, :].rearrange("p (r j) -> p r j", j=8),
                                               ALU.mult, ALU.mult).then_inc(s_act, 1)

            def combine(n, u):
                dve.wait_ge(s_ga[u], 16 * TOPE * (n // 2 + 1))
                xt = x[:, n, :]
                for k in range(TOPE):
                    nc.vector.scalar_tensor_tensor(xt, yg[:, u, k], wt[:, n, k:k + 1], xt,
                                                   ALU.mult, ALU.add).then_inc(s_cch if k < TOPE - 1 else s_cmb, 1)
                    if k < TOPE - 1:
                        dve.wait_ge(s_cch, (TOPE - 1) * n + k + 1)

            def add_shared(n, u):
                dve.wait_ge(s_dn, RT + n + 1)
                xt = x[:, n, :]
                nc.vector.scalar_tensor_tensor(xt, bank[6 + u][:, :], FP4_SCALE, xt, ALU.mult,
                                               ALU.add).then_inc(s_sh, 1)

            for e in range(3):
                decode(e, e, 32)
            dve.wait_ge(s_zero, 1)
            for j in range(NE - 3):
                gate_times_up(j, j % 2)
                decode(j + 3, 3, 32 * (NE - 3))
            with dve.Fori((NE - 3) // 2, RT // 2) as m:
                for u in range(2):
                    gate_times_up(2 * m + u, u)
            for n in range(NT):
                gate_times_up(RT + n, n % 2)
                if n >= 1:
                    add_shared(n - 1, (n - 1) % 2)
                if n >= 2:
                    dve.wait_ge(s_sh, n - 1)
                    combine(n - 2, n % 2)
            add_shared(NT - 1, 1)
            dve.wait_ge(s_sh, NT)
            combine(NT - 2, 0)
            combine(NT - 1, 1)

        @block.scalar
        def _(act):
            def copy_xT(j, u):
                act.wait_ge(s_tx, j + 1)
                nc.scalar.copy(xT[:, u, :], bank[0][:, :]).then_inc(s_xT, 1)

            def silu(j, u):
                act.wait_ge(s_gu, j + 1)
                nc.scalar.activation(sg[:, u, :], bank[2 + u][:, 0:I], ACT.Silu, scale=FP4_SCALE).then_inc(s_sg, 1)

            def copy_aT(j, u):
                act.wait_ge(s_ta, j + 1)
                nc.scalar.copy(aT[:, u, :], bank[1][:, :]).then_inc(s_aT, 1)

            def copy_y(j, u, first=False):
                act.wait_ge(s_dn, j + 1)
                if not first:
                    act.wait_ge(s_st[u], 16 * (j // 2))
                nc.scalar.copy(yt[:, u, :], bank[6 + u][:, :]).then_inc(s_y, 1)

            copy_xT(0, 0)
            copy_xT(1, 1)
            silu(0, 0)

            def pair(m, y=True, first=False):
                for u in (1, 0):
                    j = 2 * m + 2 - u
                    copy_xT(j + 1, 1 - u)
                    copy_aT(j - 1, 1 - u)
                    silu(j, u)
                    if y:
                        copy_y(j - 1, 1 - u, first)

            pair(0, first=True)
            with act.Fori(1, RT // 2) as m:
                pair(m)
            with act.Fori(RT // 2, (ALL - 2) // 2) as m:
                pair(m, y=False)
            copy_aT(ALL - 2, 0)
            silu(ALL - 1, 1)
            copy_aT(ALL - 1, 1)

        @block.tensor
        def _(pe):
            def transpose_rows(j, u, first=False):
                pe.wait_ge(s_row[u], 16 * (j // 2 + 1))
                if not first:
                    pe.wait_ge(s_xT, j)
                for b in range(4):
                    last = nc.tensor.transpose(bank[0][:, b * P:(b + 1) * P], rows[:, u, b * P:(b + 1) * P], ident[:, :])
                last.then_inc(s_tx, 1)

            def gate_up(j, u, first=False):
                e = pe.value_load(tile_e[0:1, bass.ds(j, 1)], min_val=0, max_val=E)
                pe.wait_ge(s_xT, j + 1)
                pe.wait_ge(s_W, e + 1)
                if not first:
                    pe.wait_ge(s_act, j - 1)
                for half in range(2):
                    for b in range(4):
                        last = nc.tensor.matmul(bank[2 + 2 * half + u][:, 0:I], xT[:, u, b * P:(b + 1) * P],
                                                W[:, e % 2, b, half * I:(half + 1) * I],
                                                start=(b == 0), stop=(b == 3))
                last.then_inc(s_gu, 1)

            def transpose_act(j, u, first=False):
                pe.wait_ge(s_act, j + 1)
                if not first:
                    pe.wait_ge(s_aT, j)
                for b in range(4):
                    last = nc.tensor.transpose(bank[1][:, b * P:(b + 1) * P], act_r[:, u, b * P:(b + 1) * P], ident[:, :])
                last.then_inc(s_ta, 1)

            def down(j, u, bank_free=None):
                e = pe.value_load(tile_e[0:1, bass.ds(j, 1)], min_val=0, max_val=E)
                pe.wait_ge(s_aT, j + 1)
                if bank_free:
                    pe.wait_ge(*bank_free)
                for b in range(4):
                    last = nc.tensor.matmul(bank[6 + u][:, :], aT[:, u, b * P:(b + 1) * P],
                                            W[:, e % 2, b, GU:NW], start=(b == 0), stop=(b == 3))
                last.then_inc(s_dn, 1)

            def pair(m, free):
                for u in (1, 0):
                    j = 2 * m + 2 - u
                    transpose_rows(j + 1, 1 - u)
                    transpose_act(j - 1, 1 - u, first=(free is None and u == 1))
                    gate_up(j, u)
                    down(j - 1, 1 - u, free(j - 1) if free else None)

            transpose_rows(0, 0, first=True)
            transpose_rows(1, 1)
            gate_up(0, 0, first=True)
            pair(0, None)
            with pe.Fori(1, RT // 2) as m:
                pair(m, lambda j: (s_y, j - 1))
            pair(RT // 2, lambda j: (s_y, j - 1))
            with pe.Fori(RT // 2 + 1, (ALL - 2) // 2) as m:
                pair(m, lambda j: (s_sh, j - RT - 1))
            transpose_act(ALL - 2, 0)
            gate_up(ALL - 1, 1)
            down(ALL - 2, 0, (s_sh, NT - 3))
            transpose_act(ALL - 1, 1)
            down(ALL - 1, 1, (s_sh, NT - 2))


def kernel(x, ctx_512, L0_attn_wq, L0_attn_wk, L0_attn_wv, L0_attn_wo, L0_xattn_Wq, L0_xattn_Wk,
           L0_xattn_gamma_raw, L0_ffn_gate_w, L0_ffn_gate_up_packed, L0_ffn_gate_up_scales,
           L0_ffn_down_packed, L0_ffn_down_scales, L0_ffn_shared_gate_up_packed,
           L0_ffn_shared_gate_up_scales, L0_ffn_shared_down_packed, L0_ffn_shared_down_scales):
    import concourse.bacc as bacc
    from concourse.bass_utils import run_bass_kernel_spmd

    A = np.asarray

    def lhs(w):
        return np.ascontiguousarray(w.reshape(KC, P, -1).transpose(1, 0, 2))

    wq = A(L0_attn_wq).reshape(D, G, 2, DH // 2, 2).transpose(0, 2, 4, 1, 3).reshape(D, H * DH)
    wk = A(L0_attn_wk).reshape(D, G, DH // 2, 2).transpose(0, 3, 1, 2).reshape(D, G * DH)

    def with_shared(routed, shared):
        return np.concatenate([A(routed), A(shared)[None]], axis=0)

    def pad_rows(w):
        out = np.zeros((w.shape[0], WR, w.shape[2]), w.dtype)
        out[:, :w.shape[1]] = w
        return out

    packed = np.concatenate([with_shared(L0_ffn_gate_up_packed, L0_ffn_shared_gate_up_packed),
                             pad_rows(with_shared(L0_ffn_down_packed, L0_ffn_shared_down_packed))], axis=2)
    scales = np.concatenate([
        np.repeat(with_shared(L0_ffn_gate_up_scales, L0_ffn_shared_gate_up_scales), P // 8, axis=1),
        pad_rows(np.repeat(with_shared(L0_ffn_down_scales, L0_ffn_shared_down_scales), P // 8, axis=1))], axis=2)

    inv = (1.0 / np.float32(10000.0) ** (np.arange(0, DH, 2, dtype=np.float32) / DH)).astype(np.float32)
    ang = inv[:, None] * np.arange(S, dtype=np.float32)[None, :]
    cst = np.zeros((P, NCST), np.float32)
    cst[:, IOTA:IOTA + E] = np.arange(E)
    cst[:, M128:M128 + E] = P * np.arange(E)
    cst[:, REG:REG + E] = RG * np.arange(E)
    cst[:, PAD:PAD + E] = RG * np.arange(E) + np.arange(P)[:, None]
    cst[:, LE:LE + E * E] = np.tril(np.ones((E, E))).reshape(1, -1)
    cst[:, JV:JV + RT] = np.arange(RT)
    cst[:, TAIL:TAIL + NT] = E * RG + P * np.arange(NT)
    arrays = {
        "x": A(x).reshape(NT * P, D),
        "ctxT": np.ascontiguousarray(A(ctx_512).transpose(0, 2, 1)),
        "wq": lhs(wq), "wk": lhs(wk), "wv": lhs(A(L0_attn_wv)), "wo": lhs(A(L0_attn_wo)),
        "xWq": np.ascontiguousarray(A(L0_xattn_Wq).T), "xWk": np.ascontiguousarray(A(L0_xattn_Wk).T),
        "gamma": np.broadcast_to(A(L0_xattn_gamma_raw).reshape(1, 1), (P, 1)).copy(),
        "gate": lhs(A(L0_ffn_gate_w).T.reshape(WR, 8, E).transpose(1, 0, 2)),
        "packed": packed.view(np.uint32), "scales": scales,
        "cos": np.tile(np.cos(ang), (G, 1)).astype(np.float32),
        "sin": np.tile(np.sin(ang), (G, 1)).astype(np.float32),
        "ident": np.eye(P, dtype=np.float32),
        "earlier": np.triu(np.ones((P, P), np.float32), 1),
        "cst": cst,
    }
    nc = bacc.Bacc("TRN2", target_bir_lowering=False, num_devices=1)
    aps = [nc.dram_tensor(f"in_{k}", v.shape, mybir.dt.from_np(v.dtype), kind="ExternalInput").ap()
           for k, v in arrays.items()]
    out = nc.dram_tensor("out", (NT * P, D), F32, kind="ExternalOutput").ap()
    build_program(nc, *aps, out)
    r = run_bass_kernel_spmd(nc, [{f"in_{k}": v for k, v in arrays.items()}], core_ids=[0])
    return r.results[0]["out"].reshape(B, S, D)
```
